# Optimizing a Trainium2 kernel written in Bass

```python
import numpy as np
import jax
import jax.numpy as jnp

def _softmax(x, axis=-1):
    return jax.nn.softmax(x, axis=axis)
def _gelu(x):
    return jax.nn.gelu(x, approximate=True)
def _silu(x):
    return jax.nn.silu(x)
def _sigmoid(x):
    return jax.nn.sigmoid(x)
def _layernorm(x, axis=-1, eps=1e-5):
    m = jnp.mean(x, axis=axis, keepdims=True)
    v = jnp.var(x, axis=axis, keepdims=True)
    return (x - m) / jnp.sqrt(v + eps)
def _scatter_add(tgt, idx, src, axis=0):
    return tgt.at[idx].add(src)
def _segment_sum(src, seg, n):
    return jax.ops.segment_sum(src, seg, n)

kernel_name = 'mk_conv_attn_hybrid_d2_conv_nhwc128_cf4e64'

def setup_inputs(seed: int = 0):
    np.random.seed(seed)
    _w = jnp.asarray
    def _rec_inputs():
        import jax
        import jax.numpy as jnp
        _gk = jax.random.key(seed)
        x = -0.0005153 + 1.001 * jax.random.normal(jax.random.fold_in(_gk, 1), (8, 56, 56, 128), jnp.float32)
        return x
    x = _rec_inputs()
    def _L0_conv_setup():
        import jax, jax.numpy as jnp
        import numpy as np
        KH = KW = 3
        PAD = 1
        DIL = 1
        GROUP = 4
        OFFSET_SCALE = 1.0
        P = KH * KW

        def bilinear_sample(img, iy, ix, H, W):
            x0 = jnp.floor(ix)
            y0 = jnp.floor(iy)
            wx1 = ix - x0
            wy1 = iy - y0

            def corner(yf, xf, wgt):
                valid = (yf >= 0) & (yf < H) & (xf >= 0) & (xf < W)
                idx = jnp.clip(yf, 0, H - 1).astype(jnp.int32) * W + jnp.clip(xf, 0, W - 1).astype(jnp.int32)
                v = jax.vmap(lambda im, i: im[i])(img, idx)
                return v * (wgt * valid)[..., None]
            return corner(y0, x0, (1 - wy1) * (1 - wx1)) + corner(y0, x0 + 1, (1 - wy1) * wx1) + corner(y0 + 1, x0, wy1 * (1 - wx1)) + corner(y0 + 1, x0 + 1, wy1 * wx1)

        def dcn_core(x_proj, offset, mask_sm):
            N, H, W, C = x_proj.shape
            Hin, Win = (H + 2 * PAD, W + 2 * PAD)
            Cg = C // GROUP
            pad = jnp.pad(x_proj, ((0, 0), (PAD, PAD), (PAD, PAD), (0, 0)))
            img = pad.reshape(N, Hin, Win, GROUP, Cg).transpose(0, 3, 1, 2, 4).reshape(N * GROUP, Hin * Win, Cg)
            ref_x = (jnp.arange(W, dtype=jnp.float32) + DIL * (KW - 1) // 2 + 0.5) / Win
            ref_y = (jnp.arange(H, dtype=jnp.float32) + DIL * (KH - 1) // 2 + 0.5) / Hin
            gx = jnp.arange(KW, dtype=jnp.float32) * DIL - DIL * (KW - 1) // 2
            gy = jnp.arange(KH, dtype=jnp.float32) * DIL - DIL * (KH - 1) // 2
            gxx, gyy = jnp.meshgrid(gx, gy, indexing='ij')
            gpx = (gxx / Win).reshape(P)
            gpy = (gyy / Hin).reshape(P)
            loc_x = ref_x[None, None, :, None, None] + gpx[None, None, None, None, :] * OFFSET_SCALE + offset[..., 0] * (OFFSET_SCALE / Win)
            loc_y = ref_y[None, :, None, None, None] + gpy[None, None, None, None, :] * OFFSET_SCALE + offset[..., 1] * (OFFSET_SCALE / Hin)
            ix = (loc_x * Win - 0.5).transpose(0, 3, 1, 2, 4).reshape(N * GROUP, H * W * P)
            iy = (loc_y * Hin - 0.5).transpose(0, 3, 1, 2, 4).reshape(N * GROUP, H * W * P)
            samp = bilinear_sample(img, iy, ix, Hin, Win)
            samp = samp.reshape(N, GROUP, H, W, P, Cg)
            return jnp.einsum('nghwpc,nhwgp->nhwgc', samp, mask_sm).reshape(N, H, W, C)

        def layer_norm(z, g, b, eps=1e-05):
            m = z.mean(-1, keepdims=True)
            v = ((z - m) ** 2).mean(-1, keepdims=True)
            return (z - m) / jnp.sqrt(v + eps) * g + b
        key = jax.random.key(seed)
        ks = jax.random.split(key, 12)
        N, H, W, C, G, R = (8, 56, 56, 128, GROUP, 4)

        def w(k, shp, s=0.02):
            return jax.random.normal(k, shp, jnp.float32) * s
        return dict(x=jax.random.normal(ks[0], (N, H, W, C), jnp.float32), w_in=w(ks[1], (C, C)), b_in=jnp.zeros((C,), jnp.float32), dw_w=w(ks[2], (C, 1, KH, KW)), dw_b=jnp.zeros((C,), jnp.float32), bn_g=jnp.ones((C,), jnp.float32), bn_b=jnp.zeros((C,), jnp.float32), bn_m=w(ks[3], (C,), 0.1), bn_v=jax.random.uniform(ks[4], (C,), jnp.float32, 0.5, 1.5), w_off=w(ks[5], (C, G * P * 2)), b_off=jnp.zeros((G * P * 2,), jnp.float32), w_msk=w(ks[6], (C, G * P)), b_msk=jnp.zeros((G * P,), jnp.float32), w_out=w(ks[7], (C, C)), b_out=jnp.zeros((C,), jnp.float32), ln1_g=jnp.ones((C,), jnp.float32), ln1_b=jnp.zeros((C,), jnp.float32), w_fc1=w(ks[8], (C, R * C)), b_fc1=jnp.zeros((R * C,), jnp.float32), w_fc2=w(ks[9], (R * C, C)), b_fc2=jnp.zeros((C,), jnp.float32), ln2_g=jnp.ones((C,), jnp.float32), ln2_b=jnp.zeros((C,), jnp.float32), gamma1=jnp.ones((C,), jnp.float32), gamma2=jnp.ones((C,), jnp.float32))
    _L0_conv_all = _L0_conv_setup()
    _L0_conv_in = {k: v for k, v in _L0_conv_all.items() if k in ('w_in', 'b_in', 'dw_w', 'dw_b', 'bn_g', 'bn_b', 'bn_m', 'bn_v', 'w_off', 'b_off', 'w_msk', 'b_msk', 'w_out', 'b_out', 'ln1_g', 'ln1_b', 'w_fc1', 'b_fc1', 'w_fc2', 'b_fc2', 'ln2_g', 'ln2_b', 'gamma1', 'gamma2', )}
    del _L0_conv_all

    def _L1_attn_setup():
        import jax, jax.numpy as jnp
        import numpy as np
        B, S, H, A = (8, 1024, 128, 16)
        key = jax.random.key(seed)
        ks = jax.random.split(key, 5)
        scale = 1.0 / np.sqrt(2 * H)
        return {'x': jax.random.normal(ks[0], (B, S, H), dtype=jnp.float32), 'W1': jax.random.normal(ks[1], (2 * H, A), dtype=jnp.float32) * scale, 'b1': jax.random.normal(ks[2], (A,), dtype=jnp.float32) * scale, 'w2': jax.random.normal(ks[3], (A, 1), dtype=jnp.float32) * (1.0 / np.sqrt(A)), 'b2': jax.random.normal(ks[4], (1,), dtype=jnp.float32) * (1.0 / np.sqrt(A))}
    _L1_attn_all = _L1_attn_setup()
    _L1_attn_in = {k: v for k, v in _L1_attn_all.items() if k in ('W1', 'b1', 'w2', 'b2', )}
    del _L1_attn_all

    def _L1_ffn_setup():
        import jax, jax.numpy as jnp
        import numpy as np
        B, S, D, E, H, O, K = (512, 2048, 128, 64, 512, 128, 8)
        key = jax.random.key(seed)
        k0, k1, k2, k3 = jax.random.split(key, 4)
        x = jax.random.normal(k0, (B, S, D), dtype=jnp.float32)
        gate_w = jax.random.normal(k1, (E, D), dtype=jnp.float32) * (1.0 / np.sqrt(D))
        gate_b = jnp.zeros((E,), dtype=jnp.float32)
        weight1 = jax.random.uniform(k2, (E, D + 1, H), dtype=jnp.float32, minval=-1.0, maxval=1.0) * (1.0 / np.sqrt(D + 1))
        weight2 = jax.random.uniform(k3, (E, H + 1, O), dtype=jnp.float32, minval=-1.0, maxval=1.0) * (1.0 / np.sqrt(H + 1))
        return {'x': x, 'gate_w': gate_w, 'gate_b': gate_b, 'weight1': weight1, 'weight2': weight2}
    _L1_ffn_all = _L1_ffn_setup()
    _L1_ffn_in = {k: v for k, v in _L1_ffn_all.items() if k in ('gate_w', 'gate_b', 'weight1', 'weight2', )}
    del _L1_ffn_all

    return {
        "x": x,
        "L0_conv_w_in": _L0_conv_in["w_in"],
        "L0_conv_b_in": _L0_conv_in["b_in"],
        "L0_conv_dw_w": _L0_conv_in["dw_w"],
        "L0_conv_dw_b": _L0_conv_in["dw_b"],
        "L0_conv_bn_g": _L0_conv_in["bn_g"],
        "L0_conv_bn_b": _L0_conv_in["bn_b"],
        "L0_conv_bn_m": _L0_conv_in["bn_m"],
        "L0_conv_bn_v": _L0_conv_in["bn_v"],
        "L0_conv_w_off": _L0_conv_in["w_off"],
        "L0_conv_b_off": _L0_conv_in["b_off"],
        "L0_conv_w_msk": _L0_conv_in["w_msk"],
        "L0_conv_b_msk": _L0_conv_in["b_msk"],
        "L0_conv_w_out": _L0_conv_in["w_out"],
        "L0_conv_b_out": _L0_conv_in["b_out"],
        "L0_conv_ln1_g": _L0_conv_in["ln1_g"],
        "L0_conv_ln1_b": _L0_conv_in["ln1_b"],
        "L0_conv_w_fc1": _L0_conv_in["w_fc1"],
        "L0_conv_b_fc1": _L0_conv_in["b_fc1"],
        "L0_conv_w_fc2": _L0_conv_in["w_fc2"],
        "L0_conv_b_fc2": _L0_conv_in["b_fc2"],
        "L0_conv_ln2_g": _L0_conv_in["ln2_g"],
        "L0_conv_ln2_b": _L0_conv_in["ln2_b"],
        "L0_conv_gamma1": _L0_conv_in["gamma1"],
        "L0_conv_gamma2": _L0_conv_in["gamma2"],
        "L1_attn_W1": _L1_attn_in["W1"],
        "L1_attn_b1": _L1_attn_in["b1"],
        "L1_attn_w2": _L1_attn_in["w2"],
        "L1_attn_b2": _L1_attn_in["b2"],
        "L1_ffn_gate_w": _L1_ffn_in["gate_w"],
        "L1_ffn_gate_b": _L1_ffn_in["gate_b"],
        "L1_ffn_weight1": _L1_ffn_in["weight1"],
        "L1_ffn_weight2": _L1_ffn_in["weight2"],
    }

def reference(x, L0_conv_w_in, L0_conv_b_in, L0_conv_dw_w, L0_conv_dw_b, L0_conv_bn_g, L0_conv_bn_b, L0_conv_bn_m, L0_conv_bn_v, L0_conv_w_off, L0_conv_b_off, L0_conv_w_msk, L0_conv_b_msk, L0_conv_w_out, L0_conv_b_out, L0_conv_ln1_g, L0_conv_ln1_b, L0_conv_w_fc1, L0_conv_b_fc1, L0_conv_w_fc2, L0_conv_b_fc2, L0_conv_ln2_g, L0_conv_ln2_b, L0_conv_gamma1, L0_conv_gamma2, L1_attn_W1, L1_attn_b1, L1_attn_w2, L1_attn_b2, L1_ffn_gate_w, L1_ffn_gate_b, L1_ffn_weight1, L1_ffn_weight2):
    import jax
    import jax.numpy as jnp
    def _L0_conv_ref(x, w_in, b_in, dw_w, dw_b, bn_g, bn_b, bn_m, bn_v, w_off, b_off, w_msk, b_msk, w_out, b_out, ln1_g, ln1_b, w_fc1, b_fc1, w_fc2, b_fc2, ln2_g, ln2_b, gamma1, gamma2):
        import jax, jax.numpy as jnp
        import numpy as np
        KH = KW = 3
        PAD = 1
        DIL = 1
        GROUP = 4
        OFFSET_SCALE = 1.0
        P = KH * KW

        def bilinear_sample(img, iy, ix, H, W):
            x0 = jnp.floor(ix)
            y0 = jnp.floor(iy)
            wx1 = ix - x0
            wy1 = iy - y0

            def corner(yf, xf, wgt):
                valid = (yf >= 0) & (yf < H) & (xf >= 0) & (xf < W)
                idx = jnp.clip(yf, 0, H - 1).astype(jnp.int32) * W + jnp.clip(xf, 0, W - 1).astype(jnp.int32)
                v = jax.vmap(lambda im, i: im[i])(img, idx)
                return v * (wgt * valid)[..., None]
            return corner(y0, x0, (1 - wy1) * (1 - wx1)) + corner(y0, x0 + 1, (1 - wy1) * wx1) + corner(y0 + 1, x0, wy1 * (1 - wx1)) + corner(y0 + 1, x0 + 1, wy1 * wx1)

        def dcn_core(x_proj, offset, mask_sm):
            N, H, W, C = x_proj.shape
            Hin, Win = (H + 2 * PAD, W + 2 * PAD)
            Cg = C // GROUP
            pad = jnp.pad(x_proj, ((0, 0), (PAD, PAD), (PAD, PAD), (0, 0)))
            img = pad.reshape(N, Hin, Win, GROUP, Cg).transpose(0, 3, 1, 2, 4).reshape(N * GROUP, Hin * Win, Cg)
            ref_x = (jnp.arange(W, dtype=jnp.float32) + DIL * (KW - 1) // 2 + 0.5) / Win
            ref_y = (jnp.arange(H, dtype=jnp.float32) + DIL * (KH - 1) // 2 + 0.5) / Hin
            gx = jnp.arange(KW, dtype=jnp.float32) * DIL - DIL * (KW - 1) // 2
            gy = jnp.arange(KH, dtype=jnp.float32) * DIL - DIL * (KH - 1) // 2
            gxx, gyy = jnp.meshgrid(gx, gy, indexing='ij')
            gpx = (gxx / Win).reshape(P)
            gpy = (gyy / Hin).reshape(P)
            loc_x = ref_x[None, None, :, None, None] + gpx[None, None, None, None, :] * OFFSET_SCALE + offset[..., 0] * (OFFSET_SCALE / Win)
            loc_y = ref_y[None, :, None, None, None] + gpy[None, None, None, None, :] * OFFSET_SCALE + offset[..., 1] * (OFFSET_SCALE / Hin)
            ix = (loc_x * Win - 0.5).transpose(0, 3, 1, 2, 4).reshape(N * GROUP, H * W * P)
            iy = (loc_y * Hin - 0.5).transpose(0, 3, 1, 2, 4).reshape(N * GROUP, H * W * P)
            samp = bilinear_sample(img, iy, ix, Hin, Win)
            samp = samp.reshape(N, GROUP, H, W, P, Cg)
            return jnp.einsum('nghwpc,nhwgp->nhwgc', samp, mask_sm).reshape(N, H, W, C)

        def layer_norm(z, g, b, eps=1e-05):
            m = z.mean(-1, keepdims=True)
            v = ((z - m) ** 2).mean(-1, keepdims=True)
            return (z - m) / jnp.sqrt(v + eps) * g + b
        N, H, W, C = x.shape
        xp = x @ w_in + b_in
        h = x.transpose(0, 3, 1, 2)
        h = jax.lax.conv_general_dilated(h, dw_w, (1, 1), ((PAD, PAD), (PAD, PAD)), feature_group_count=C, dimension_numbers=('NCHW', 'OIHW', 'NCHW')) + dw_b[None, :, None, None]
        h = (h - bn_m[None, :, None, None]) * (bn_g / jnp.sqrt(bn_v + 1e-05))[None, :, None, None] + bn_b[None, :, None, None]
        h = jax.nn.gelu(h.transpose(0, 2, 3, 1), approximate=False)
        offset = (h @ w_off + b_off).reshape(N, H, W, GROUP, P, 2)
        mask = jax.nn.softmax((h @ w_msk + b_msk).reshape(N, H, W, GROUP, P), axis=-1)
        y = dcn_core(xp, offset, mask) @ w_out + b_out
        x = x + gamma1 * layer_norm(y, ln1_g, ln1_b)
        m = jax.nn.gelu(x @ w_fc1 + b_fc1, approximate=False) @ w_fc2 + b_fc2
        x = x + gamma2 * layer_norm(m, ln2_g, ln2_b)
        return x

    def _L1_attn_ref(x, W1, b1, w2, b2):
        import jax, jax.numpy as jnp
        import numpy as np
        B, S, H, A = (8, 1024, 128, 16)
        h = x.shape[-1]
        f = jnp.einsum('bih,ha->bia', x, W1[:h])
        g = jnp.einsum('bjh,ha->bja', x, W1[h:])
        t = jnp.tanh(f[:, :, None, :] + g[:, None, :, :] + b1)
        scores = jnp.einsum('bija,a->bij', t, w2[:, 0]) + b2[0]
        n_seq = x.shape[1]
        flag = jnp.tril(jnp.ones((n_seq, n_seq), dtype=x.dtype), -1)[None, :, :]
        e = jnp.exp(scores) * flag
        denom = jnp.sum(e, axis=-1, keepdims=True) + 1e-10
        w = e / denom
        return jnp.einsum('bij,bjh->bih', w, x)

    def _L1_ffn_ref(x, gate_w, gate_b, weight1, weight2):
        import jax, jax.numpy as jnp
        import numpy as np
        B, S, D, E, H, O, K = (512, 2048, 128, 64, 512, 128, 8)
        Bn, Sn, Dn = x.shape
        logits = jnp.einsum('bsd,ed->bse', x, gate_w) + gate_b
        probs = jax.nn.softmax(logits, axis=1)
        vals, idx = jax.lax.top_k(probs.transpose(0, 2, 1), K)
        topv = vals.transpose(0, 2, 1)
        topi = idx.transpose(0, 2, 1)
        flat_idx = topi.reshape(Bn, K * E)
        gathered = jnp.take_along_axis(x, flat_idx[:, :, None], axis=1)
        gathered = gathered.reshape(Bn, K, E, Dn)
        pooled = jnp.einsum('bked,bke->bed', gathered, topv)
        ones = jnp.ones((E, Bn, 1), dtype=x.dtype)
        h = jnp.concatenate([pooled.transpose(1, 0, 2), ones], axis=-1)
        h = jax.nn.gelu(jnp.einsum('ebd,edh->ebh', h, weight1), approximate=False)
        h = jnp.concatenate([h, ones], axis=-1)
        out = jnp.einsum('ebh,eho->ebo', h, weight2)
        out = out.transpose(1, 0, 2)
        weighted = jnp.einsum('beo,bke->bkeo', out, topv).reshape(Bn, K * E, O)
        outputs = jnp.zeros((Bn, Sn, O), dtype=x.dtype)
        outputs = outputs.at[jnp.arange(Bn)[:, None], flat_idx].add(weighted)
        return outputs

    def _gn(v, G=32, eps=1e-5):
        B_, H_, W_, C_ = v.shape
        g = v.reshape(B_, H_, W_, G, C_ // G)
        m = jnp.mean(g, axis=(1, 2, 4), keepdims=True)
        s = jnp.var(g, axis=(1, 2, 4), keepdims=True)
        return ((g - m) / jnp.sqrt(s + eps)).reshape(v.shape)

    def _ln_c(v, eps=1e-6):
        m = jnp.mean(v, axis=-1, keepdims=True)
        s = jnp.var(v, axis=-1, keepdims=True)
        return (v - m) / jnp.sqrt(s + eps)

    def _ln_t(v, eps=1e-5):
        m = jnp.mean(v, axis=-1, keepdims=True)
        s = jnp.var(v, axis=-1, keepdims=True)
        return (v - m) / jnp.sqrt(s + eps)

    def _to_tokens(v):
        B_, H_, W_, C_ = v.shape
        return v.reshape(B_, H_ * W_, C_)
    def _from_tokens(t, like):
        return t.reshape(like.shape)

    x = _L0_conv_ref(x, L0_conv_w_in, L0_conv_b_in, L0_conv_dw_w, L0_conv_dw_b, L0_conv_bn_g, L0_conv_bn_b, L0_conv_bn_m, L0_conv_bn_v, L0_conv_w_off, L0_conv_b_off, L0_conv_w_msk, L0_conv_b_msk, L0_conv_w_out, L0_conv_b_out, L0_conv_ln1_g, L0_conv_ln1_b, L0_conv_w_fc1, L0_conv_b_fc1, L0_conv_w_fc2, L0_conv_b_fc2, L0_conv_ln2_g, L0_conv_ln2_b, L0_conv_gamma1, L0_conv_gamma2)
    t = _to_tokens(x)
    t = t + _L1_attn_ref(_ln_t(t), L1_attn_W1, L1_attn_b1, L1_attn_w2, L1_attn_b2)
    t = t + _L1_ffn_ref(_ln_t(t), L1_ffn_gate_w, L1_ffn_gate_b, L1_ffn_weight1, L1_ffn_weight2)
    x = _from_tokens(t, x)
    return x


_drawn_inputs = setup_inputs


def setup_inputs(seed=0):
    import zlib

    import numpy as np

    out = dict(_drawn_inputs(seed))
    spreads = {'L0_conv_b_in': (0.0, 0.1),
     'L0_conv_dw_b': (0.0, 0.8),
     'L0_conv_bn_g': (1.0, 0.6),
     'L0_conv_bn_b': (0.0, 0.8),
     'L0_conv_b_off': (0.0, 0.674),
     'L0_conv_b_msk': (0.0, 0.8),
     'L0_conv_b_out': (0.0, 0.1),
     'L0_conv_ln1_g': (1.0, 0.2),
     'L0_conv_ln1_b': (0.0, 0.1),
     'L0_conv_b_fc1': (0.0, 0.1),
     'L0_conv_b_fc2': (0.0, 0.1),
     'L0_conv_ln2_g': (1.0, 0.2),
     'L0_conv_ln2_b': (0.0, 0.1),
     'L0_conv_gamma1': (1.0, 0.2),
     'L0_conv_gamma2': (1.0, 0.2),
     'L1_ffn_gate_b': (0.0, 0.1)}
    factors = {'L0_conv_dw_w': 8.0,
     'L0_conv_bn_m': 8.0,
     'L0_conv_bn_v': 8.0,
     'L0_conv_w_off': 8.0,
     'L0_conv_w_msk': 8.0,
     'L1_attn_W1': 6.904,
     'L1_attn_b1': 8.0,
     'L1_attn_w2': 6.517,
     'L1_ffn_gate_w': 8.0,
     'L1_ffn_weight1': 8.0,
     'L1_ffn_weight2': 8.0}
    for name, (base, spread) in spreads.items():
        noise = np.random.default_rng([zlib.crc32(name.encode()), seed]).standard_normal(out[name].shape)
        drawn = base * np.exp(spread * noise) if base else spread * noise
        out[name] = jnp.asarray(drawn.astype(out[name].dtype))
    for name, factor in factors.items():
        out[name] = (out[name] * factor).astype(out[name].dtype)
    return out
```

```python
import concourse.bass as bass
from concourse import mybir
from contextlib import ExitStack

F32 = mybir.dt.float32
I32 = mybir.dt.int32
U32 = mybir.dt.uint32
ALU = mybir.AluOpType
ACT = mybir.ActivationFunctionType
AX_X = mybir.AxisListType.X

P = 128
C = 128
H = W = 56
S = H * W
GROUPS, CG, TAPS = 4, 32, 9
HP = H + 2
PATCHES = HP * HP
NPATCH = (PATCHES + P - 1) // P
SUB = 64
NSUB = S // SUB
SAMPLES = GROUPS // 2 * TAPS
BAND_ROWS = 8
BAND = BAND_ROWS * W
NBAND = H // BAND_ROWS
BAND_SUBS = BAND // SUB
PARAMS = GROUPS // 2 * TAPS * 3
NBLK = (S + P - 1) // P
A = 16
ROWS8 = P // A
CHUNK = 1024
E = 64
K_TOP = 8
HID = 512
EPS = 1e-5
GATHER_SLOTS = 4
FLOOR_MAGIC = 8388608.0
RSQRT_MAGIC = 1597463007.0


def blk_rows(k):
    return min(P, S - k * P)


def patch_rows(i):
    return min(P, PATCHES - i * P)


def chunks_of(k):
    tiles = k + 1
    n = -(-tiles * P // CHUNK)
    cuts = [tiles * i // n for i in range(n + 1)]
    return [list(range(cuts[i], cuts[i + 1])) for i in range(n)]


def chunk_width(tiles):
    return sum(blk_rows(j) for j in tiles)


CHUNK_INDEX = {}
UNIT_INDEX = {}
QUAD_INDEX = {}
for _k in range(NBLK):
    for _c, _tiles in enumerate(chunks_of(_k)):
        CHUNK_INDEX[_k, _c] = len(CHUNK_INDEX)
        for _s in range(blk_rows(_k) // ROWS8):
            UNIT_INDEX[_k, _c, _s] = len(UNIT_INDEX)
        for _p in range(-(-len(_tiles) // 4)):
            QUAD_INDEX[_k, _c, _p] = len(QUAD_INDEX)
CHUNKS, UNITS, QUADS = len(CHUNK_INDEX), len(UNIT_INDEX), len(QUAD_INDEX)


def gather_slot(t):
    return t % GATHER_SLOTS if t < NSUB - 1 else 1


SLOT_USES = [sum(gather_slot(t) == b for t in range(NSUB)) for b in range(GATHER_SLOTS)]


def slot_use(t):
    return sum(gather_slot(u) == gather_slot(t) for u in range(t))


def last_user(t):
    for u in range(t - 1, t - NSUB - 1, -1):
        if gather_slot(u % NSUB) == gather_slot(t):
            return u


def prepare_tasks():
    out = []
    for g in range(NBAND):
        out += [(g + .15, ("image_in", g)), (g + .45, ("project_in", g))]
    for t in range(NPATCH):
        out.append((7.05 + t * .28, ("patches", t)))
    for g in range(NBAND):
        due = (g + 1) * BAND_SUBS / 2
        out += [(due + .05, ("conv", g)), (due + .3, ("offsets", g)), (due + .75, ("weights", g))]
    return out


def attend_tasks(k, begin, span):
    units = [u for u in UNIT_INDEX if u[0] == k]
    n = len(units)
    out = []
    per = blk_rows(k) // ROWS8
    for i, u in enumerate(units):
        out.append((begin + span * i / n, ("unit", *u)))
    for c in range(len(chunks_of(k))):
        done = (c + 1) * per
        late = begin + span * done / n
        d = span / n
        if c == len(chunks_of(k)) - 1:
            d = span / 32
        out += [(late + 2.1 * d, ("exp", k, c)), (late + 4.1 * d, ("values", k, c))]
    out += [(begin + span + .20, ("finish", k)), (begin + span + .30, ("route", k))]
    return out


def image_order(with_next):
    tasks = []
    for k in range(NBLK):
        tasks.append((k - .01, ("x_in", k)))
        for i, name in enumerate(("sample", "sample2", "turn", "mix", "turn_mid", "hidden", "mlp_out", "turn_norm", "keys")):
            at = k + .02 + .11 * i
            if name == "sample":
                tasks.append((at, ("sample", 2 * k)))
            elif name == "sample2":
                if 2 * k + 1 < NSUB:
                    tasks.append((at, ("sample", 2 * k + 1)))
            else:
                tasks.append((at, (name, k)))
        tasks += attend_tasks(k, k + 1, 1.0)
    if with_next:
        tasks += prepare_tasks()
    return [t for _, t in sorted(tasks, key=lambda x: x[0])]


class Line:

    def __init__(self, sem, per_image, step=1):
        self.sem, self.per_image, self.step = sem, per_image, step

    @property
    def lead(self):
        return self.per_image * self.step

    def after(self, image, i):
        return image * self.lead + (self.lead + (i + 1) * self.step)

    def free(self, image, i, ring):
        return self.after(image, i - ring if i >= ring else -1)


def first_layer_and_attention(nc, io, x2_d, xln2_d, logits_d, patches_d, images):
    with ExitStack() as ctx:
        def sb(name, shape, dt=F32):
            return ctx.enter_context(nc.sbuf_tensor(name, shape, dt))

        def ps(name, shape):
            return ctx.enter_context(nc.psum_tensor(name, shape, F32))

        def sem(name):
            return ctx.enter_context(nc.semaphore(name))

        ident = sb("ident", [P, P])
        earlier = sb("earlier", [P, P])
        score_place = sb("score_place", [P, 4, 32])
        score_w = sb("score_w", [P, 4, 32])
        grid = sb("grid", [P, BAND_SUBS, 2 * SAMPLES])
        base_index = sb("base_index", [P, SAMPLES])
        chan = sb("chan", [P, 6])
        dw = sb("dw", [P, TAPS])
        taps = sb("taps", [P, TAPS, C])
        bn = sb("bn", [P, 2])
        w_in = sb("w_in", [C, C])
        w_par = sb("w_par", [C, 2, PARAMS])
        b_par = sb("b_par", [P, PARAMS])
        w_out = sb("w_out", [P, 2, C])
        w_fc1 = sb("w_fc1", [C, HID])
        w_fc2 = sb("w_fc2", [P, HID // P, C])
        rows = sb("rows", [1, HID + 2 * C])
        ones = sb("ones", [1, P])
        affine = sb("affine", [P, 6, C])
        w_key = sb("w_key", [C, ROWS8, A])
        w_q = sb("w_q", [C, A])
        w_query = sb("w_query", [C, ROWS8, ROWS8, A])
        tiny = sb("tiny", [P, 3])
        gate_w = sb("gate_w", [C, E])
        gate_b = sb("gate_b", [E, 1])
        x_band = sb("x_band", [112, 2, 4, C])
        x_pad = sb("x_pad", [C, HP, HP])
        xp_flat = sb("xp_flat", [C, PATCHES + HP + 2])
        patch = sb("patch", [P, 2, GROUPS, 4, CG])
        h_band = sb("h_band", [C, BAND])
        xy = sb("xy", [P, BAND_SUBS, SAMPLES, 2])
        cell = sb("cell", [P, BAND_SUBS, SAMPLES, 2])
        above = sb("above", [P, BAND_SUBS, SAMPLES, 2])
        flat = sb("flat", [P, BAND_SUBS, SAMPLES])
        mask = sb("mask", [P, BAND_SUBS, SAMPLES])
        upper = sb("upper", [P, BAND_SUBS, SAMPLES])
        lower = sb("lower", [P, BAND_SUBS, SAMPLES])
        stat = sb("stat", [P, BAND_SUBS * 2])
        index = sb("index", [P, NBAND, BAND_SUBS * SAMPLES], I32)
        corner_w = sb("corner_w", [P, NBAND, BAND_SUBS, SAMPLES * 4])
        gathered = sb("gathered", [P, GATHER_SLOTS, SAMPLES * 4 * CG])
        product = sb("product", [P, SAMPLES * 4, CG])
        y = sb("y", [P, 2, 2 * CG])
        yT = sb("yT", [P, P])
        x_tok = sb("x_tok", [P, 2, C])
        mid = sb("mid", [P, C])
        midT = sb("midT", [C, P])
        hid = sb("hid", [P, HID // P, P])
        x1 = sb("x1", [P, 5, C])
        ln_a = sb("ln_a", [P, C])
        ln_b = sb("ln_b", [P, C])
        lnT = sb("lnT", [C, P])
        bst = sb("bst", [P, 6])
        mv = sb("mv", [P, 2])
        var = sb("var", [P, 1])
        seed = sb("seed", [P, 1], I32)
        rstd = sb("rstd", [P, 1])
        newton = sb("newton", [P, 2])
        key_rep = sb("key_rep", [P, S])
        query = sb("query", [P, NBLK * A])
        values = sb("values", [P, NBLK, C + 1])
        tanh = sb("tanh", [P, 4, CHUNK])
        expo = sb("expo", [P, 2, CHUNK])
        expoT = sb("expoT", [P, 2, 4, P])
        den = sb("den", [P, 2])
        x2 = sb("x2", [P, 2, C])
        xln2 = sb("xln2", [P, 2, C])
        xln2T = sb("xln2T", [C, P])
        logit = sb("logit", [E, 2, P])

        score_ps = ps("score_ps", [P, 2, CHUNK])
        turn_ps = ps("turn_ps", [P, 4, P])
        value_ps = ps("value_ps", [P, 512])
        chain_ps = ps("chain_ps", [P, 512])
        side_ps = ps("side_ps", [P, 512])

        consts_in = sem("consts_in")
        consts_ready = sem("consts_ready")
        prologue_go = sem("prologue_go")
        pool_step = sem("pool_step")
        pe_step = sem("pe_step")
        x_band_in = [Line(sem(f"x_band_in{i}"), (NBAND + 1 - i) // 2, 16) for i in range(2)]
        patches_out = [Line(sem(f"patches_out{i}"), (NPATCH + 1 - i) // 2, 16) for i in range(2)]
        x_tok_in = [Line(sem(f"x_tok_in{i}"), (NBLK + 1 - i) // 2, 16) for i in range(2)]
        block_out = [Line(sem(f"block_out{i}"), (NBLK + 1 - i) // 2, 48) for i in range(2)]
        gather_done = [sem(f"gather_done{i}") for i in range(GATHER_SLOTS)]

        def line(name, per_image):
            return Line(sem(name), per_image)

        band_turned = line("band_turned", NBAND)
        band_copied = line("band_copied", NBAND)
        in_projected = line("in_projected", NBAND)
        in_copied = line("in_copied", NBAND)
        patch_turned = line("patch_turned", NPATCH)
        patch_ready = line("patch_ready", NPATCH)
        conv_done = line("conv_done", NBAND)
        h_ready = line("h_ready", NBAND)
        params_done = line("params_done", NBAND)
        index_ready = line("index_ready", NBAND)
        mask_shifted = line("mask_shifted", NBAND)
        mask_exp = line("mask_exp", NBAND)
        sampled = line("sampled", NSUB)
        y_turned = line("y_turned", NBLK)
        y_copied = line("y_copied", NBLK)
        mixed = line("mixed", NBLK)
        mid_ready = line("mid_ready", NBLK)
        mid_turned = line("mid_turned", NBLK)
        mid_copied = line("mid_copied", NBLK)
        hid_done = line("hid_done", NBLK)
        gelu_done = line("gelu_done", NBLK)
        mlp_done = line("mlp_done", NBLK)
        norm_ready = line("norm_ready", NBLK)
        norm_turned = line("norm_turned", NBLK)
        norm_copied = line("norm_copied", NBLK)
        keys_done = line("keys_done", NBLK)
        keys_copied = line("keys_copied", NBLK)
        tanh_done = line("tanh_done", UNITS)
        scored = line("scored", UNITS)
        exp_done = line("exp_done", CHUNKS)
        masked = line("masked", NBLK)
        exp_turned = line("exp_turned", QUADS)
        exp_copied = line("exp_copied", QUADS)
        quad_used = line("quad_used", QUADS)
        x2_ready = line("x2_ready", NBLK)
        ln2_ready = line("ln2_ready", NBLK)
        ln2_turned = line("ln2_turned", NBLK)
        ln2_copied = line("ln2_copied", NBLK)
        logits_done = line("logits_done", NBLK)
        logits_copied = line("logits_copied", NBLK)

        PREP_SIDE = 2 * NBAND + NPATCH + NBAND
        side_read = sem("side_read")
        BODY_SIDE = PREP_SIDE + 2 * NBLK

        block = ctx.enter_context(nc.Block())

        def walk(engine, task, begin=lambda: None):
            def image(n, odd, last=False):
                begin()
                for name in image_order(not last):
                    task(n, None if last else n + 1, odd, name)

            begin()
            for _, name in sorted(prepare_tasks(), key=lambda x: x[0]):
                task(-1, 0, True, name)
            if images > 2:
                with engine.Fori(0, images - 2, 2) as n:
                    image(n, False)
                    image(n + 1, True)
            image(images - 2, False)
            image(images - 1, True, last=True)

        @block.sync
        def _(sp):
            names = ["ident", "earlier", "score_place", "grid", "base_index", "chan", "dw", "w_in", "w_par",
                     "b_par", "w_out", "w_fc1", "w_fc2", "rows", "affine", "w_key", "w_q", "tiny", "gate_w", "gate_b"]
            tiles = dict(ident=ident, earlier=earlier, score_place=score_place, grid=grid, base_index=base_index,
                         chan=chan, dw=dw, w_in=w_in, w_par=w_par, b_par=b_par, w_out=w_out, w_fc1=w_fc1,
                         w_fc2=w_fc2, rows=rows, affine=affine, w_key=w_key, w_q=w_q, tiny=tiny, gate_w=gate_w, gate_b=gate_b)
            for name in names:
                sp.dma_start(tiles[name][:], io[name]).then_inc(consts_in, 16)
            for ln in (*x_band_in, *patches_out, *x_tok_in, *block_out):
                nc.sync.sem_inc(ln.sem, ln.lead)

            def task(n, m, odd, name):
                what, i = name[:2]
                b = i % 2
                if what == "image_in":
                    sp.wait_ge(band_turned.sem, band_turned.free(m, i, 2))
                    sp.dma_start(x_band[:, b], io["x"][bass.ds(m * S + i * BAND, BAND), :]
                                 .rearrange("(q p) c -> p q c", p=112)).then_inc(x_band_in[b].sem, 16)
                elif what == "patches":
                    sp.wait_ge(patch_ready.sem, patch_ready.after(m, i))
                    if i < 2 and not (isinstance(n, int) and n < 0):
                        sp.wait_ge(sampled.sem, sampled.after(n, -1))
                    sp.dma_start(patches_d[int(not odd)][i * P:i * P + patch_rows(i), :],
                                 patch[:patch_rows(i), b].rearrange("p g k c -> p (g k c)")).then_inc(patches_out[b].sem, 16)
                elif what == "x_in":
                    sp.wait_ge(mid_ready.sem, mid_ready.free(n, i, 2))
                    sp.dma_start(x_tok[:blk_rows(i), b], io["x"][bass.ds(n * S + i * P, blk_rows(i)), :])\
                        .then_inc(x_tok_in[b].sem, 16)
                elif what == "route":
                    r = blk_rows(i)
                    sp.wait_ge(ln2_ready.sem, ln2_ready.after(n, i))
                    sp.dma_start(x2_d[bass.ds(n * S + i * P, r), :], x2[:r, b]).then_inc(block_out[b].sem, 16)
                    sp.dma_start(xln2_d[bass.ds(n * S + i * P, r), :], xln2[:r, b]).then_inc(block_out[b].sem, 16)
                    sp.wait_ge(logits_copied.sem, logits_copied.after(n, i))
                    sp.dma_start(logits_d[bass.ds(n * E, E), i * P:i * P + r], logit[:, b, :r])\
                        .then_inc(block_out[b].sem, 16)

            walk(sp, task)
            for ln in block_out:
                sp.wait_ge(ln.sem, ln.after(images - 1, ln.per_image - 1))
            for ln in patches_out:
                sp.wait_ge(ln.sem, ln.after(images - 1, ln.per_image - 1))

        @block.gpsimd
        def _(pool):
            def gathers(n, odd):
                for ln in patches_out:
                    pool.wait_ge(ln.sem, ln.after(n, ln.per_image - 1))
                    nc.gpsimd.sem_inc(pool_step, 1)
                for t in range(NSUB):
                    g, tt = divmod(t, BAND_SUBS)
                    b = gather_slot(t)
                    if tt == 0:
                        pool.wait_ge(index_ready.sem, index_ready.after(n, g))
                        nc.gpsimd.sem_inc(pool_step, 1)
                    pool.wait_ge(sampled.sem, sampled.after(n, last_user(t)))
                    nc.gpsimd.sem_inc(pool_step, 1)
                    for j in range(SAMPLES):
                        at = tt * SAMPLES + j
                        pool.indirect_dma_start(
                            gathered[:, b, j * 4 * CG:(j + 1) * 4 * CG], None, patches_flat[int(odd)],
                            bass.IndirectOffsetOnAxis(ap=index[:, g, at:at + 1].bitcast(U32), axis=0),
                        ).then_inc(gather_done[b], 16)

            patches_flat = [d.rearrange("n (g k) -> (n g) k", g=GROUPS) for d in patches_d]
            if images > 2:
                with pool.Fori(0, images - 2, 2) as n:
                    gathers(n, False)
                    gathers(n + 1, True)
            gathers(images - 2, False)
            gathers(images - 1, True)

        @block.vector
        def _(dve):
            v = nc.vector

            def settle():
                return v.drain()

            for ln in (band_copied, in_copied, patch_ready, index_ready, mask_shifted, sampled, y_copied, mid_ready,
                       mid_copied, norm_ready, norm_copied, keys_copied, masked, exp_copied, x2_ready, ln2_ready,
                       ln2_copied, logits_copied):
                v.sem_inc(ln.sem, ln.lead)
            v.memset(x_pad[:], 0.0)
            v.memset(xp_flat[:], 0.0)
            v.memset(w_query[:], 0.0)
            v.memset(ones[:], 1.0)
            v.memset(y[:], 0.0)
            v.memset(values[:, :, C:C + 1], 1.0)
            settle()
            dve.wait_ge(consts_in, 16 * 20)
            for t in range(TAPS):
                v.tensor_scalar(taps[:, t], ident[:], dw[:, t:t + 1], None, ALU.mult)
            for i in range(ROWS8):
                v.tensor_copy(w_query[:, i, i], w_q[:])
            v.tensor_scalar(score_w[:], score_place[:], tiny[:, 1:2], None, ALU.mult)
            v.tensor_tensor(grid[:], grid[:], b_par[:, None, 0:2 * SAMPLES].to_broadcast([P, BAND_SUBS, 2 * SAMPLES]),
                            ALU.add)
            for s in (0, 3):
                v.tensor_tensor(affine[:, s], affine[:, s], affine[:, s + 2], ALU.mult)
                v.tensor_tensor(affine[:, s + 1], affine[:, s + 1], affine[:, s + 2], ALU.mult)
            v.tensor_tensor(bn[:, 1:2], chan[:, 1:2], chan[:, 4:5], ALU.subtract)
            v.tensor_scalar(var[:], chan[:, 5:6], EPS, None, ALU.add)
            settle()

            def rsqrt(r):
                v.tensor_scalar(seed[:r], var[:r].bitcast(I32), 1, None, ALU.logical_shift_right)
                settle()
                v.tensor_scalar(rstd[:r].bitcast(I32), seed[:r], -1.0, RSQRT_MAGIC, ALU.mult, ALU.add)
                settle()
                for _ in range(3):
                    v.scalar_tensor_tensor(newton[:r, 0:1], rstd[:r], var[:r], rstd[:r], ALU.mult, ALU.mult)
                    settle()
                    v.tensor_scalar(newton[:r, 1:2], newton[:r, 0:1], -0.5, 1.5, ALU.mult, ALU.add)
                    settle()
                    v.tensor_tensor(rstd[:r], rstd[:r], newton[:r, 1:2], ALU.mult)
                    settle()

            def moments(src, r):
                v.bn_stats(bst[:r], src)
                settle()
                v.bn_aggr(mv[:r], bst[:r])
                settle()
                v.tensor_scalar(var[:r], mv[:r, 1:2], EPS, None, ALU.add)
                settle()
                rsqrt(r)

            rsqrt(P)
            v.tensor_tensor(bn[:, 0:1], rstd[:], chan[:, 2:3], ALU.mult)
            settle()
            v.scalar_tensor_tensor(bn[:, 1:2], bn[:, 1:2], bn[:, 0:1], chan[:, 3:4], ALU.mult, ALU.add)
            settle().then_inc(consts_ready, 1)

            def wait(ln, image, i):
                dve.wait_ge(ln.sem, ln.after(image, i))

            def add_norm(src, out, residual, s, r):
                moments(src, r)
                v.scalar_tensor_tensor(ln_a[:r], src, mv[:r, 0:1], affine[:r, s], ALU.subtract, ALU.mult)
                v.tensor_tensor(ln_b[:r], residual, affine[:r, s + 1], ALU.add)
                settle()

            def task(n, m, odd, name):
                what, i = name[:2]
                b = i % 2
                if what == "image_in":
                    rs = slice(1 + i * BAND_ROWS, 1 + (i + 1) * BAND_ROWS)
                    wait(band_turned, m, i)
                    wait(conv_done, m, -1)
                    v.tensor_copy(x_pad[:, rs, 1:W + 1], side_ps[:, :BAND].rearrange("p (a b) -> p a b", b=W))
                    settle().then_inc(band_copied.sem, 1)
                    v.sem_inc(side_read, 1)
                elif what == "project_in":
                    rs = slice(1 + i * BAND_ROWS, 1 + (i + 1) * BAND_ROWS)
                    wait(in_projected, m, i)
                    wait(patch_turned, m, -1)
                    v.tensor_scalar(xp_flat[:, :PATCHES].rearrange("p (a b) -> p a b", b=HP)[:, rs, 1:W + 1], side_ps[:, :BAND].rearrange("p (a b) -> p a b", b=W),
                                    chan[:, 0:1], None, ALU.add)
                    settle().then_inc(in_copied.sem, 1)
                    v.sem_inc(side_read, 1)
                elif what == "patches":
                    wait(patch_turned, m, i)
                    dve.wait_ge(patches_out[b].sem, patches_out[b].after(m, i // 2 - 1))
                    v.tensor_copy(patch[:patch_rows(i), b].rearrange("p g k c -> p k g c"),
                                  side_ps[:patch_rows(i)].rearrange("p (k g c) -> p k g c", k=4, g=GROUPS))
                    settle().then_inc(patch_ready.sem, 1)
                    v.sem_inc(side_read, 1)
                elif what == "offsets":
                    wait(params_done, m, i)
                    par = side_ps[:, :BAND_SUBS * PARAMS].rearrange("p (t c) -> p t c", c=PARAMS)
                    xyf = xy[:].rearrange("p t s a -> p t (s a)")
                    v.tensor_tensor(xyf, par[:, :, :2 * SAMPLES], grid[:], ALU.add)
                    v.tensor_tensor(mask[:], par[:, :, 2 * SAMPLES:],
                                    b_par[:, None, 2 * SAMPLES:].to_broadcast([P, BAND_SUBS, SAMPLES]), ALU.add)
                    settle().then_inc(side_read, 1)
                    mask9 = mask[:].rearrange("p t (g s) -> p (t g) s", s=TAPS)
                    v.tensor_reduce(stat[:], mask9, AX_X, ALU.max)
                    if i:
                        v.tensor_scalar(xy[:, :, :, 1], xy[:, :, :, 1], float(BAND_ROWS * i), None, ALU.add)
                    settle()
                    v.tensor_tensor(mask9, mask9, stat[:].unsqueeze(2).to_broadcast([P, BAND_SUBS * 2, TAPS]),
                                    ALU.subtract)
                    v.tensor_scalar(xy[:], xy[:], float(HP - 1), 0.0, ALU.min, ALU.max)
                    settle().then_inc(mask_shifted.sem, 1)
                    v.tensor_scalar(cell[:], xy[:], FLOOR_MAGIC, FLOOR_MAGIC, ALU.add, ALU.subtract)
                    settle()
                    v.tensor_tensor(above[:], cell[:], xy[:], ALU.is_gt)
                    settle()
                    v.tensor_tensor(cell[:], cell[:], above[:], ALU.subtract)
                    settle()
                    v.tensor_tensor(xy[:], xy[:], cell[:], ALU.subtract)
                    v.scalar_tensor_tensor(flat[:], cell[:, :, :, 1], float(HP), cell[:, :, :, 0], ALU.mult, ALU.add)
                    settle()
                    v.scalar_tensor_tensor(index[:, i].rearrange("p (t s) -> p t s", s=SAMPLES), flat[:],
                                           float(GROUPS), base_index[:, None, :].to_broadcast([P, BAND_SUBS, SAMPLES]),
                                           ALU.mult, ALU.add)
                    settle().then_inc(index_ready.sem, 1)
                elif what == "weights":
                    wait(mask_exp, m, i)
                    mask9 = mask[:].rearrange("p t (g s) -> p (t g) s", s=TAPS)
                    v.tensor_reduce(stat[:], mask9, AX_X, ALU.add)
                    settle()
                    v.reciprocal(stat[:], stat[:])
                    settle()
                    v.tensor_tensor(mask9, mask9, stat[:].unsqueeze(2).to_broadcast([P, BAND_SUBS * 2, TAPS]), ALU.mult)
                    settle()
                    cw = corner_w[:, i].rearrange("p t (s k) -> p t s k", k=4)
                    v.tensor_tensor(lower[:], mask[:], xy[:, :, :, 1], ALU.mult)
                    settle()
                    v.tensor_tensor(upper[:], mask[:], lower[:], ALU.subtract)
                    v.tensor_tensor(cw[:, :, :, 3], lower[:], xy[:, :, :, 0], ALU.mult)
                    settle()
                    v.tensor_tensor(cw[:, :, :, 1], upper[:], xy[:, :, :, 0], ALU.mult)
                    v.tensor_tensor(cw[:, :, :, 2], lower[:], cw[:, :, :, 3], ALU.subtract)
                    settle()
                    v.tensor_tensor(cw[:, :, :, 0], upper[:], cw[:, :, :, 1], ALU.subtract)
                    settle()
                elif what == "sample":
                    slot = gather_slot(i)
                    g, tt = divmod(i, BAND_SUBS)
                    each = 16 * SAMPLES
                    dve.wait_ge(gather_done[slot], n * (SLOT_USES[slot] * each) + (slot_use(i) + 1) * each)
                    wait(y_turned, n, i // 2 - 1)
                    v.tensor_tensor(product[:], gathered[:, slot].rearrange("p (a c) -> p a c", c=CG),
                                    corner_w[:, g, tt].unsqueeze(2).to_broadcast([P, SAMPLES * 4, CG]), ALU.mult)
                    settle()
                    v.tensor_reduce(y[:, b].rearrange("p (g c) -> p g c", c=CG),
                                    product[:].rearrange("p (g k) c -> p g c k", g=2), AX_X, ALU.add)
                    settle().then_inc(sampled.sem, 1)
                elif what == "turn":
                    wait(y_turned, n, i)
                    wait(mixed, n, i - 1)
                    v.tensor_copy(yT[:], chain_ps[:, :P])
                    settle().then_inc(y_copied.sem, 1)
                elif what == "mix":
                    r = blk_rows(i)
                    wait(mixed, n, i)
                    dve.wait_ge(x_tok_in[b].sem, x_tok_in[b].after(n, i // 2))
                    wait(mid_turned, n, i - 1)
                    add_norm(chain_ps[:r, :C], mid, x_tok[:r, b], 0, r)
                    v.scalar_tensor_tensor(mid[:r], ln_a[:r], rstd[:r], ln_b[:r], ALU.mult, ALU.add)
                    settle().then_inc(mid_ready.sem, 1)
                elif what == "turn_mid":
                    r = blk_rows(i)
                    wait(mid_turned, n, i)
                    wait(hid_done, n, i - 1)
                    v.tensor_copy(midT[:, :r], chain_ps[:, :r])
                    settle().then_inc(mid_copied.sem, 1)
                elif what == "mlp_out":
                    r = blk_rows(i)
                    wait(mlp_done, n, i)
                    if i == 0:
                        wait(quad_used, n, -1)
                    add_norm(chain_ps[:r, :C], x1, mid[:r], 3, r)
                    v.scalar_tensor_tensor(x1[:r, i % 5], ln_a[:r], rstd[:r], ln_b[:r], ALU.mult, ALU.add)
                    settle()
                    moments(x1[:r, i % 5], r)
                    v.tensor_scalar(values[:r, i, :C], x1[:r, i % 5], mv[:r, 0:1], rstd[:r], ALU.subtract, ALU.mult)
                    settle().then_inc(norm_ready.sem, 1)
                elif what == "turn_norm":
                    r = blk_rows(i)
                    wait(norm_turned, n, i)
                    wait(keys_done, n, i - 1)
                    v.tensor_copy(lnT[:, :r], chain_ps[:, :r])
                    settle().then_inc(norm_copied.sem, 1)
                elif what == "keys":
                    r = blk_rows(i)
                    wait(keys_done, n, i)
                    if i == 0:
                        wait(tanh_done, n, -1)
                    v.tensor_copy(key_rep[:, i * P:i * P + r], chain_ps[:, :r])
                    v.tensor_scalar(query[:, i * A:i * A + r // ROWS8], chain_ps[:, P:P + r // ROWS8], tiny[:, 0:1],
                                    None, ALU.add)
                    settle().then_inc(keys_copied.sem, 1)
                elif what == "values":
                    k, c = name[1:]
                    r = blk_rows(k)
                    tiles = chunks_of(k)[c]
                    ci = CHUNK_INDEX[k, c]
                    wait(exp_done, n, ci)
                    if c == len(chunks_of(k)) - 1:
                        w = chunk_width(tiles)
                        diagonal = expo[:r, ci % 2, w - r:w]
                        v.tensor_tensor(diagonal, diagonal, earlier[:r, :r], ALU.mult)
                        settle().then_inc(masked.sem, 1)
                    for q in range(-(-len(tiles) // 4)):
                        quad = tiles[4 * q:4 * q + 4]
                        pi = QUAD_INDEX[k, c, q]
                        wait(exp_turned, n, pi)
                        dve.wait_ge(quad_used.sem, quad_used.free(n, pi, 2))
                        for z, rows_ in column_runs(quad):
                            v.tensor_copy(expoT[:rows_, pi % 2, z[0]:z[1], :r],
                                          turn_ps[:rows_, z[0]:z[1], :r])
                        settle().then_inc(exp_copied.sem, 1)
                elif what == "finish":
                    r = blk_rows(i)
                    wait(quad_used, n, QUAD_INDEX[i, len(chunks_of(i)) - 1, -(-len(chunks_of(i)[-1]) // 4) - 1])
                    dve.wait_ge(block_out[b].sem, block_out[b].after(n, i // 2 - 1))
                    wait(ln2_turned, n, i - 1)
                    v.tensor_scalar(den[:r, 0:1], value_ps[:r, C:C + 1], 1e-10, None, ALU.add)
                    settle()
                    v.reciprocal(den[:r, 1:2], den[:r, 0:1])
                    settle()
                    v.scalar_tensor_tensor(x2[:r, b], value_ps[:r, :C], den[:r, 1:2], x1[:r, i % 5],
                                           ALU.mult, ALU.add)
                    settle().then_inc(x2_ready.sem, 1)
                    moments(x2[:r, b], r)
                    v.tensor_scalar(xln2[:r, b], x2[:r, b], mv[:r, 0:1], rstd[:r], ALU.subtract, ALU.mult)
                    settle().then_inc(ln2_ready.sem, 1)
                elif what == "route":
                    r = blk_rows(i)
                    wait(ln2_turned, n, i)
                    wait(logits_done, n, i - 1)
                    v.tensor_copy(xln2T[:, :r], side_ps[:, :r])
                    settle().then_inc(ln2_copied.sem, 1)
                    v.sem_inc(side_read, 1)
                    wait(logits_done, n, i)
                    v.tensor_scalar(logit[:, b, :r], side_ps[:E, :r], gate_b[:], None, ALU.add)
                    settle().then_inc(logits_copied.sem, 1)
                    v.sem_inc(side_read, 1)

            walk(dve, task)

        @block.scalar
        def _(act):
            for ln in (h_ready, mask_exp, gelu_done, tanh_done, exp_done):
                nc.scalar.sem_inc(ln.sem, ln.lead)
            act.wait_ge(consts_ready, 1)

            def wait(ln, image, i):
                act.wait_ge(ln.sem, ln.after(image, i))

            def task(n, m, odd, name):
                what, i = name[:2]
                if what == "conv":
                    wait(conv_done, m, i)
                    wait(params_done, m, i - 1)
                    nc.scalar.activation(h_band[:], side_ps[:, :BAND], ACT.Gelu, bias=bn[:, 1:2], scale=bn[:, 0:1])\
                        .then_inc(h_ready.sem, 1)
                elif what == "offsets":
                    wait(mask_shifted, m, i)
                    nc.scalar.activation(mask[:], mask[:], ACT.Exp).then_inc(mask_exp.sem, 1)
                elif what == "hidden":
                    r = blk_rows(i)
                    wait(hid_done, n, i)
                    wait(mlp_done, n, i - 1)
                    nc.scalar.activation(hid[:, :, :r], chain_ps[:].rearrange("p (a b) -> p a b", b=P)[:, :, :r],
                                         ACT.Gelu).then_inc(gelu_done.sem, 1)
                elif what == "unit":
                    k, c, s = name[1:]
                    ui = UNIT_INDEX[k, c, s]
                    if (c, s) == (0, 0):
                        wait(keys_copied, n, k)
                    act.wait_ge(scored.sem, scored.free(n, ui, 4))
                    tiles = chunks_of(k)[c]
                    w = chunk_width(tiles)
                    lo = tiles[0] * P
                    col = k * A + row_group(k, s)
                    nc.scalar.activation(tanh[:, ui % 4, :w], key_rep[:, lo:lo + w], ACT.Tanh,
                                         bias=query[:, col:col + 1]).then_inc(tanh_done.sem, 1)
                elif what == "exp":
                    k, c = name[1:]
                    r = blk_rows(k)
                    ci = CHUNK_INDEX[k, c]
                    w = chunk_width(chunks_of(k)[c])
                    wait(scored, n, UNIT_INDEX[k, c, r // ROWS8 - 1])
                    if ci >= 2:
                        wait(exp_turned, n, last_quad_of_chunk(ci - 2))
                    else:
                        wait(exp_turned, n, -1)
                    nc.scalar.activation(expo[:r, ci % 2, :w], score_ps[:r, ci % 2, :w], ACT.Exp, bias=tiny[:r, 2:3])\
                        .then_inc(exp_done.sem, 1)

            walk(act, task)

        @block.tensor
        def _(pe):
            mm = nc.tensor.matmul
            for ln in (band_turned, in_projected, patch_turned, conv_done, params_done, y_turned, mixed, mid_turned,
                       hid_done, mlp_done, norm_turned, keys_done, scored, exp_turned, quad_used, ln2_turned,
                       logits_done):
                nc.tensor.sem_inc(ln.sem, ln.lead)
            pe.wait_ge(consts_ready, 1)
            side_uses = [0]
            last_conv = []

            def wait(ln, image, i):
                pe.wait_ge(ln.sem, ln.after(image, i))

            def side_free(n):
                if last_conv:
                    wait(h_ready, *last_conv.pop())
                first = isinstance(n, int) and n < 0
                if first and side_uses[0] == 0:
                    side_uses[0] += 1
                    return
                before = side_uses[0] if first else n * BODY_SIDE + (PREP_SIDE + side_uses[0])
                pe.wait_ge(side_read, before)
                side_uses[0] += 1

            def turn(out, src, r, cols=P):
                if r < P or cols < P:
                    nc.tensor.sem_inc(pe_step, 1)
                return mm(out, src, ident[:r, :r], is_transpose=True, start=True, stop=True)

            def task(n, m, odd, name):
                what, i = name[:2]
                b = i % 2
                if what == "image_in":
                    side_free(n)
                    pe.wait_ge(x_band_in[b].sem, x_band_in[b].after(m, i // 2))
                    for q in range(4):
                        last = turn(side_ps[:, q * 112:(q + 1) * 112], x_band[:, b, q], 112)
                    last.then_inc(band_turned.sem, 1)
                elif what == "project_in":
                    side_free(n)
                    wait(band_copied, m, i)
                    mm(side_ps[:, :BAND], w_in[:], x_pad[:, 1 + i * BAND_ROWS:1 + (i + 1) * BAND_ROWS, 1:W + 1],
                       start=True, stop=True).then_inc(in_projected.sem, 1)
                elif what == "patches":
                    side_free(n)
                    wait(in_copied, m, min(NBAND - 1, ((i * P + P + HP) // HP - 1) // BAND_ROWS))
                    for k in range(4):
                        dy, dx = divmod(k, 2)
                        at = i * P + dy * HP + dx
                        last = turn(side_ps[:patch_rows(i), k * C:(k + 1) * C], xp_flat[:, at:at + patch_rows(i)], P,
                                    patch_rows(i))
                    last.then_inc(patch_turned.sem, 1)
                elif what == "conv":
                    side_free(n)
                    wait(band_copied, m, min(i + 1, NBAND - 1))
                    for t in range(TAPS):
                        dy, dx = divmod(t, 3)
                        last = mm(side_ps[:, :BAND], taps[:, t],
                                  x_pad[:, i * BAND_ROWS + dy:(i + 1) * BAND_ROWS + dy, dx:dx + W],
                                  start=t == 0, stop=t == TAPS - 1)
                    last.then_inc(conv_done.sem, 1)
                    side_uses[0] -= 1
                    last_conv.append((m, i))
                elif what == "offsets":
                    side_free(n)
                    wait(h_ready, m, i)
                    for t in range(BAND_SUBS):
                        for half in range(2):
                            last = mm(side_ps[half * SUB:(half + 1) * SUB, t * PARAMS:(t + 1) * PARAMS],
                                      h_band[:, t * SUB:(t + 1) * SUB], w_par[:, half], start=True, stop=True)
                    last.then_inc(params_done.sem, 1)
                elif what == "turn":
                    wait(sampled, n, min(2 * i + 1, NSUB - 1))
                    wait(keys_copied, n, i - 1)
                    turn(chain_ps[:, :P], y[:].rearrange("p a b -> p (a b)"), P).then_inc(y_turned.sem, 1)
                elif what == "mix":
                    r = blk_rows(i)
                    wait(y_copied, n, i)
                    last = mm(chain_ps[:r, :C], ones[:, :r], rows[:, HID:HID + C], start=True, stop=False)
                    for s in range(r // SUB):
                        part = slice(s * SUB, (s + 1) * SUB)
                        for half in range(2):
                            last = mm(chain_ps[part, :C], yT[part, half * SUB:(half + 1) * SUB], w_out[part, half],
                                      start=False, stop=half == 1)
                    last.then_inc(mixed.sem, 1)
                elif what == "turn_mid":
                    r = blk_rows(i)
                    wait(mid_ready, n, i)
                    turn(chain_ps[:, :r], mid[:r], r).then_inc(mid_turned.sem, 1)
                elif what == "hidden":
                    r = blk_rows(i)
                    wait(mid_copied, n, i)
                    for c in range(HID // P):
                        cols = slice(c * P, (c + 1) * P)
                        mm(chain_ps[:, c * P:c * P + r], rows[:, cols], ones[:, :r], start=True, stop=False)
                        last = mm(chain_ps[:, c * P:c * P + r], w_fc1[:, cols], midT[:, :r], start=False, stop=True)
                    last.then_inc(hid_done.sem, 1)
                elif what == "mlp_out":
                    r = blk_rows(i)
                    wait(gelu_done, n, i)
                    mm(chain_ps[:r, :C], ones[:, :r], rows[:, HID + C:], start=True, stop=False)
                    for c in range(HID // P):
                        last = mm(chain_ps[:r, :C], hid[:, c, :r], w_fc2[:, c], start=False, stop=c == HID // P - 1)
                    last.then_inc(mlp_done.sem, 1)
                elif what == "turn_norm":
                    r = blk_rows(i)
                    wait(norm_ready, n, i)
                    turn(chain_ps[:, :r], values[:r, i, :C], r).then_inc(norm_turned.sem, 1)
                elif what == "keys":
                    r = blk_rows(i)
                    wait(norm_copied, n, i)
                    mm(chain_ps[:, :r], w_key[:].rearrange("p a b -> p (a b)"), lnT[:, :r], start=True, stop=True)
                    for q in range(ROWS8):
                        last = mm(chain_ps[:, P:P + r // ROWS8], w_query[:, q].rearrange("p a b -> p (a b)"),
                                  lnT[:, q:r:ROWS8], start=q == 0, stop=q == ROWS8 - 1)
                    last.then_inc(keys_done.sem, 1)
                elif what == "unit":
                    k, c, s = name[1:]
                    r = blk_rows(k)
                    ui, ci = UNIT_INDEX[k, c, s], CHUNK_INDEX[k, c]
                    w = chunk_width(chunks_of(k)[c])
                    group = row_group(k, s)
                    col, place = divmod(group, 4)
                    if place == 0:
                        pe.wait_ge(exp_done.sem, exp_done.free(n, ci, 2))
                    wait(tanh_done, n, ui)
                    for lo in range(0, w, 512):
                        hi = min(w, lo + 512)
                        last = mm(score_ps[32 * col:32 * col + 32, ci % 2, lo:hi], score_w[:, place],
                                  tanh[:, ui % 4, lo:hi], start=place == 0, stop=place == 3)
                    last.then_inc(scored.sem, 1)
                elif what == "values":
                    k, c = name[1:]
                    r = blk_rows(k)
                    tiles = chunks_of(k)[c]
                    ci = CHUNK_INDEX[k, c]
                    n_quads = -(-len(tiles) // 4)
                    wait(exp_done, n, ci)
                    if c == len(chunks_of(k)) - 1:
                        wait(masked, n, k)
                    for q in range(n_quads + 1):
                        if q < n_quads:
                            pi = QUAD_INDEX[k, c, q]
                            pe.wait_ge(exp_copied.sem, exp_copied.after(n, pi - 1))
                            for z, j in enumerate(tiles[4 * q:4 * q + 4]):
                                at = (j - tiles[0]) * P
                                wj = blk_rows(j)
                                last = turn(turn_ps[:wj, z, :r], expo[:r, ci % 2, at:at + wj], r, wj)
                            last.then_inc(exp_turned.sem, 1)
                        if q > 0:
                            pi = QUAD_INDEX[k, c, q - 1]
                            wait(exp_copied, n, pi)
                            if c == 0 and q == 1:
                                wait(x2_ready, n, k - 1)
                            for z, j in enumerate(tiles[4 * q - 4:4 * q]):
                                wj = blk_rows(j)
                                last = mm(value_ps[:r, :C + 1], expoT[:wj, pi % 2, z, :r], values[:wj, j],
                                          start=j == 0, stop=j == k)
                            last.then_inc(quad_used.sem, 1)
                elif what == "route":
                    r = blk_rows(i)
                    side_free(n)
                    wait(ln2_ready, n, i)
                    turn(side_ps[:, :r], xln2[:r, b], r).then_inc(ln2_turned.sem, 1)
                    side_free(n)
                    wait(ln2_copied, n, i)
                    mm(side_ps[:E, :r], gate_w[:], xln2T[:, :r], start=True, stop=True).then_inc(logits_done.sem, 1)

            def begin():
                side_uses[0] = 0

            walk(pe, task, begin)


def row_group(k, s):
    cols = blk_rows(k) // 32
    return 4 * (s % cols) + s // cols


def last_quad_of_chunk(ci):
    k, c = [kc for kc, i in CHUNK_INDEX.items() if i == ci][0]
    return QUAD_INDEX[k, c, -(-len(chunks_of(k)[c]) // 4) - 1]


def column_runs(quad):
    whole = sum(blk_rows(j) == P for j in quad)
    runs = [((0, whole), P)] if whole else []
    return runs + [((z, z + 1), blk_rows(quad[z])) for z in range(whole, len(quad))]


ROW_T = 28
ROW_P = S // ROW_T
SLOTS = 4
PER = 4
LOW = -3.0e38


def route_and_experts(nc, io, xln2_d, logits_d, chosen_d, expert_d, images):
    pairs = images * E // P
    with ExitStack() as ctx:
        def sb(name, shape, dt=F32):
            return ctx.enter_context(nc.sbuf_tensor(name, shape, dt))

        def ps(name, shape):
            return ctx.enter_context(nc.psum_tensor(name, shape, F32))

        def sem(name):
            return ctx.enter_context(nc.semaphore(name))

        eye = sb("eye", [P, P])
        bias1 = sb("bias1", [P, E, HID // P])
        score = sb("score", [P, 2, S])
        prob = sb("prob", [P, S])
        chosen = sb("chosen", [P, 2, S])
        chosenT = sb("chosenT", [ROW_P, ROW_T, P])
        tokens = sb("tokens", [ROW_P, 2, 2, ROW_T, C])
        top = sb("top", [P, K_TOP])
        neg = sb("neg", [P, 1])
        total = sb("total", [P, 2])
        pooled = sb("pooled", [C, E, images])
        w1 = sb("w1", [P, SLOTS, PER, HID])
        w2 = sb("w2", [P, SLOTS, PER, HID])
        pre = sb("pre", [P, 2, PER, HID // P, images])
        act1 = sb("act1", [P, 2, PER, HID // P, images])
        outs = sb("outs", [images, 2, PER, C])

        turned_ps = ps("turned_ps", [P, 2, 4, P])
        pool_ps = ps("pool_ps", [P, 2, 512])
        hid_ps = ps("hid_ps", [P, 2, 512])
        out_ps = ps("out_ps", [P, 2, 512])

        eye_in = sem("eye_in")
        score_in = [sem(f"score_in{i}") for i in range(2)]
        tokens_in = [sem(f"tokens_in{i}") for i in range(2)]
        chosen_out = [sem(f"chosen_out{i}") for i in range(2)]
        w_in = [sem(f"expert_w_in{i}") for i in range(SLOTS)]
        expert_out = [sem(f"expert_out{i}") for i in range(2)]
        top_ready = sem("top_ready")
        prob_ready = sem("prob_ready")
        prob_used = sem("prob_used")
        chosen_ready = sem("chosen_ready")
        chosen_turned = sem("chosen_turned")
        chosen_copied = sem("chosen_copied")
        pooled_done = sem("pooled_done")
        pooled_ready = sem("pooled_ready")
        hid_done = sem("expert_hid_done")
        pre_ready = sem("pre_ready")
        act_ready = sem("act_ready")
        out_done = sem("expert_out_done")
        out_copied = sem("out_copied")
        steps = E // PER
        rounds = steps // SLOTS
        TURNS = ROW_T // 4

        block = ctx.enter_context(nc.Block())

        @block.sync
        def _(sp):
            sp.dma_start(eye[:], io["ident"]).then_inc(eye_in, 16)
            sp.dma_start(bias1[:], io["weight1"][:, C, :].rearrange("e (p c) -> p e c", c=HID // P)).then_inc(eye_in, 16)

            def load_tokens(pr):
                b = pr % 2
                sp.dma_start(score[:, b], logits_d[pr * P:(pr + 1) * P, :]).then_inc(score_in[b], 16)
                for half in range(2):
                    at = (2 * pr + half) * S
                    sp.dma_start(tokens[:, b, half], xln2_d[at:at + S, :].rearrange("(p t) c -> p t c", t=ROW_T))\
                        .then_inc(tokens_in[b], 16)

            def load_experts(first, slot):
                sp.dma_start(w1[:, slot], io["weight1"][bass.ds(first, PER), :C, :].rearrange("e p h -> p e h"))\
                    .then_inc(w_in[slot], 16)
                sp.dma_start(w2[:, slot], io["weight2"][bass.ds(first, PER), :HID, :]
                             .rearrange("e (p c) o -> p e (c o)", c=HID // P)).then_inc(w_in[slot], 16)

            for pr in range(min(2, pairs)):
                load_tokens(pr)
            for slot in range(SLOTS):
                load_experts(slot * PER, slot)
            for pr in range(pairs):
                sp.wait_ge(chosen_ready, pr + 1)
                sp.dma_start(chosen_d[pr * P:(pr + 1) * P, :], chosen[:, pr % 2]).then_inc(chosen_out[pr % 2], 16)
                if pr + 2 < pairs:
                    sp.wait_ge(pooled_done, pr + 1)
                    load_tokens(pr + 2)
            def results(it, slot):
                sp.wait_ge(out_copied, it * SLOTS + (slot + 1))
                sp.dma_start(expert_d[bass.ds(it * (SLOTS * PER) + slot * PER, PER)].rearrange("e b o -> b e o"),
                             outs[:, slot % 2]).then_inc(expert_out[slot % 2], 16)

            with sp.Fori(0, rounds - 1) as it:
                for slot in range(SLOTS):
                    results(it, slot)
                    load_experts(it * (SLOTS * PER) + (SLOTS + slot) * PER, slot)
            for slot in range(SLOTS):
                results(rounds - 1, slot)
            for b in range(2):
                sp.wait_ge(expert_out[b], 16 * steps // 2)
                if b < pairs:
                    sp.wait_ge(chosen_out[b], 16 * ((pairs + 1 - b) // 2))

        @block.vector
        def _(dve):
            v = nc.vector

            def settle():
                return v.drain()

            for pr in range(pairs):
                b = pr % 2
                dve.wait_ge(score_in[b], 16 * (pr // 2 + 1))
                v.max(top[:], score[:, b])
                settle()
                v.tensor_scalar(neg[:], top[:, 0:1], -1.0, None, ALU.mult)
                settle().then_inc(top_ready, 1)
                if pr >= 2:
                    dve.wait_ge(chosen_turned, TURNS * (pr - 1))
                    dve.wait_ge(chosen_out[b], 16 * (pr // 2))
                v.match_replace(chosen[:, b], top[:], score[:, b], LOW)
                settle()
                v.tensor_tensor(chosen[:, b], score[:, b], chosen[:, b], ALU.not_equal)
                dve.wait_ge(prob_ready, pr + 1)
                v.reciprocal(total[:, 1:2], total[:, 0:1])
                settle()
                v.scalar_tensor_tensor(chosen[:, b], prob[:], total[:, 1:2], chosen[:, b], ALU.mult, ALU.mult)
                settle().then_inc(chosen_ready, 1)
                for q in range(TURNS):
                    u = pr * TURNS + q
                    dve.wait_ge(chosen_turned, u + 1)
                    if q == 0 and pr:
                        dve.wait_ge(pooled_done, pr)
                    v.tensor_copy(chosenT[:, 4 * q:4 * q + 4], turned_ps[:ROW_P, u % 2])
                    settle().then_inc(chosen_copied, 1)
                dve.wait_ge(pooled_done, pr + 1)
                for half in range(2):
                    v.tensor_copy(pooled[:, :, 2 * pr + half], pool_ps[:, half, :E])
                settle().then_inc(pooled_ready, 1)
            dve.wait_ge(eye_in, 32)
            with dve.Fori(0, rounds) as it:
                for s in range(SLOTS):
                    b = s % 2
                    dve.wait_ge(hid_done, it * SLOTS + (s + 1))
                    v.tensor_tensor(pre[:, b].rearrange("p e c b -> p (e c) b"),
                                    hid_ps[:, b, :PER * HID // P * images].rearrange("p (a b) -> p a b", b=images),
                                    bias1[:, bass.ds(it * (SLOTS * PER) + s * PER, PER), :]
                                    .rearrange("p e c -> p (e c)").unsqueeze(2)
                                    .to_broadcast([P, PER * HID // P, images]), ALU.add)
                    settle().then_inc(pre_ready, 1)
                    dve.wait_ge(out_done, it * SLOTS + (s + 1))
                    dve.wait_ge(expert_out[b], it * (16 * SLOTS // 2) + (16 * (s // 2)))
                    v.tensor_copy(outs[:, b].rearrange("p e o -> p (e o)"), out_ps[:images, b])
                    settle().then_inc(out_copied, 1)

        @block.scalar
        def _(act):
            for pr in range(pairs):
                act.wait_ge(top_ready, pr + 1)
                if pr:
                    act.wait_ge(chosen_ready, pr)
                nc.scalar.activation(prob[:], score[:, pr % 2], ACT.Exp, bias=neg[:], accum_out=total[:, 0:1])
                nc.scalar.drain().then_inc(prob_ready, 1)
            with act.Fori(0, rounds) as it:
                for s in range(SLOTS):
                    act.wait_ge(pre_ready, it * SLOTS + (s + 1))
                    nc.scalar.activation(act1[:, s % 2], pre[:, s % 2], ACT.Gelu).then_inc(act_ready, 1)

        @block.tensor
        def _(pe):
            mm = nc.tensor.matmul
            pe.wait_ge(eye_in, 32)
            for pr in range(pairs):
                b = pr % 2
                pe.wait_ge(chosen_ready, pr + 1)
                for q in range(TURNS):
                    u = pr * TURNS + q
                    if u >= 2:
                        pe.wait_ge(chosen_copied, u - 1)
                    for z in range(4):
                        last = mm(turned_ps[:ROW_P, u % 2, z], chosen[:, b, 4 * q + z::ROW_T], eye[:],
                                  is_transpose=True, start=True, stop=True)
                    last.then_inc(chosen_turned, 1)
                pe.wait_ge(chosen_copied, (pr + 1) * TURNS)
                pe.wait_ge(tokens_in[b], 32 * (pr // 2 + 1))
                if pr:
                    pe.wait_ge(pooled_ready, pr)
                for half in range(2):
                    for t in range(ROW_T):
                        last = mm(pool_ps[:, half, :E], tokens[:, b, half, t], chosenT[:, t, half * E:(half + 1) * E],
                                  start=t == 0, stop=t == ROW_T - 1)
                last.then_inc(pooled_done, 1)
            pe.wait_ge(pooled_ready, pairs)
            with pe.Fori(0, rounds) as it:
                for s in range(SLOTS):
                    b = s % 2
                    pe.wait_ge(w_in[s], it * 32 + 32)
                    for e in range(PER):
                        for c in range(HID // P):
                            col = (e * (HID // P) + c) * images
                            last = mm(hid_ps[:, b, col:col + images], w1[:, s, e, c::HID // P],
                                      pooled[:, bass.ds(it * (SLOTS * PER) + s * PER + e, 1), :]
                                      .rearrange("p e b -> p (e b)"), start=True, stop=True)
                    last.then_inc(hid_done, 1)
                    pe.wait_ge(act_ready, it * SLOTS + (s + 1))
                    if s >= 2:
                        pe.wait_ge(out_copied, it * SLOTS + (s - 1))
                    for e in range(PER):
                        for c in range(HID // P):
                            last = mm(out_ps[:images, b, e * C:(e + 1) * C], act1[:, b, e, c], 
                                      w2[:, s, e, c * C:(c + 1) * C], start=c == 0, stop=c == HID // P - 1)
                    last.then_inc(out_done, 1)


def combine(nc, io, x2_d, chosen_d, expert_d, out, images):
    with ExitStack() as ctx:
        def sb(name, shape, dt=F32):
            return ctx.enter_context(nc.sbuf_tensor(name, shape, dt))

        def sem(name):
            return ctx.enter_context(nc.semaphore(name))

        expert = sb("expert", [E, images, C])
        bias2 = sb("bias2", [E, C])
        picked = sb("picked", [E, 2, S])
        resid = sb("resid", [ROW_P, 2, ROW_T * C])
        mix_ps = ctx.enter_context(nc.psum_tensor("mix_ps", [P, 8, 512], F32))
        expert_in = sem("expert_in")
        image_in = [sem(f"image_in{i}") for i in range(2)]
        expert_ready = sem("expert_ready")
        mixed = sem("expert_mixed")
        added = sem("added")
        out_done = [sem(f"image_out{i}") for i in range(2)]
        QUADS = ROW_T // 4
        block = ctx.enter_context(nc.Block())

        @block.sync
        def _(sp):
            sp.dma_start(expert[:], expert_d).then_inc(expert_in, 16)
            sp.dma_start(bias2[:], io["weight2"][:, HID, :]).then_inc(expert_in, 16)
            for n in range(images):
                b = n % 2
                if n >= 2:
                    sp.wait_ge(added, QUADS * (n - 1))
                    sp.wait_ge(out_done[b], 16 * (n // 2))
                sp.dma_start(picked[:, b], chosen_d[n * E:(n + 1) * E, :]).then_inc(image_in[b], 16)
                sp.dma_start(resid[:, b], x2_d[n * S:(n + 1) * S, :].rearrange("(p t) c -> p (t c)", t=ROW_T))\
                    .then_inc(image_in[b], 16)

        @block.scalar
        def _(act):
            for n in range(images):
                act.wait_ge(added, QUADS * (n + 1))
                act.dma_start(out[n * S:(n + 1) * S, :].rearrange("(p t) c -> p (t c)", t=ROW_T), resid[:, n % 2])\
                    .then_inc(out_done[n % 2], 16)
            for b in range(2):
                act.wait_ge(out_done[b], 16 * ((images + 1 - b) // 2))

        @block.vector
        def _(dve):
            v = nc.vector
            dve.wait_ge(expert_in, 32)
            v.tensor_tensor(expert[:], expert[:], bias2[:, None, :].to_broadcast([E, images, C]), ALU.add)
            v.drain().then_inc(expert_ready, 1)
            for n in range(images):
                for q in range(QUADS):
                    dve.wait_ge(mixed, n * QUADS + q + 1)
                    part = resid[:, n % 2, q * 512:(q + 1) * 512]
                    v.tensor_tensor(part, part, mix_ps[:ROW_P, (n * QUADS + q) % 8], ALU.add).then_inc(added, 1)

        @block.tensor
        def _(pe):
            pe.wait_ge(expert_ready, 1)
            for n in range(images):
                pe.wait_ge(image_in[n % 2], 32 * (n // 2 + 1))
                for q in range(QUADS):
                    u = n * QUADS + q
                    if u >= 8:
                        pe.wait_ge(added, u - 7)
                    for z in range(4):
                        last = nc.tensor.matmul(mix_ps[:ROW_P, u % 8, z * C:(z + 1) * C],
                                                picked[:, n % 2, 4 * q + z::ROW_T], expert[:, n], start=True, stop=True)
                    last.then_inc(mixed, 1)


def layout(inputs):
    import numpy as np

    def f(name):
        return np.asarray(inputs[name], dtype=np.float32)

    half, pos = np.divmod(np.arange(P), SUB)
    place = np.arange(BAND_SUBS)[None, :] * SUB + pos[:, None]
    tap = np.arange(SAMPLES) % TAPS
    grid = np.zeros((P, BAND_SUBS, SAMPLES, 2), np.float32)
    grid[..., 0] = (place % W)[..., None] + tap // 3
    grid[..., 1] = (place // W)[..., None] + tap % 3
    base = (2 * half[:, None] + np.arange(SAMPLES)[None, :] // TAPS).astype(np.float32)
    score_place = np.zeros((P, 4, 32), np.float32)
    for r in range(4):
        for q in range(ROWS8):
            score_place[q * A:(q + 1) * A, r, 8 * r + q] = 1.0
    off = f("L0_conv_w_off").reshape(C, 2, 2 * SAMPLES)
    msk = f("L0_conv_w_msk").reshape(C, 2, SAMPLES)
    b_par = np.concatenate([f("L0_conv_b_off").reshape(2, -1), f("L0_conv_b_msk").reshape(2, -1)], 1)
    w_out = f("L0_conv_w_out").reshape(2, SUB, C).transpose(1, 0, 2)
    chan = ["b_in", "dw_b", "bn_g", "bn_b", "bn_m", "bn_v"]
    affine = ["ln1_g", "ln1_b", "gamma1", "ln2_g", "ln2_b", "gamma2"]
    w1 = f("L1_attn_W1")
    arrays = {
        "x": f("x").reshape(-1, C),
        "ident": np.eye(P, dtype=np.float32),
        "earlier": np.tril(np.ones((P, P), np.float32), -1),
        "score_place": score_place,
        "grid": grid.reshape(P, BAND_SUBS, 2 * SAMPLES),
        "base_index": base,
        "chan": np.stack([f("L0_conv_" + n) for n in chan], 1),
        "dw": f("L0_conv_dw_w").reshape(C, TAPS),
        "w_in": f("L0_conv_w_in"),
        "w_par": np.concatenate([off, msk], 2),
        "b_par": np.repeat(b_par, SUB, 0),
        "w_out": np.concatenate([w_out, w_out], 0),
        "w_fc1": f("L0_conv_w_fc1"),
        "w_fc2": f("L0_conv_w_fc2").reshape(HID // P, P, C).transpose(1, 0, 2),
        "rows": np.concatenate([f("L0_conv_b_fc1"), f("L0_conv_b_out"), f("L0_conv_b_fc2")])[None],
        "affine": np.tile(np.stack([f("L0_conv_" + n) for n in affine])[None], (P, 1, 1)),
        "w_key": np.tile(w1[C:, None, :], (1, ROWS8, 1)),
        "w_q": w1[:C],
        "tiny": np.stack([np.tile(f("L1_attn_b1"), ROWS8), np.tile(f("L1_attn_w2")[:, 0], ROWS8),
                          np.tile(f("L1_attn_b2"), P)], 1),
        "gate_w": f("L1_ffn_gate_w").T,
        "gate_b": f("L1_ffn_gate_b")[:, None],
        "weight1": f("L1_ffn_weight1"),
        "weight2": f("L1_ffn_weight2"),
    }
    return {k: np.ascontiguousarray(a) for k, a in arrays.items()}


def program(nc, io, out, images):
    x2_d = nc.dram_tensor("x2_d", [images * S, C], F32, kind="Internal").ap()
    xln2_d = nc.dram_tensor("xln2_d", [images * S, C], F32, kind="Internal").ap()
    logits_d = nc.dram_tensor("logits_d", [images * E, S], F32, kind="Internal").ap()
    chosen_d = nc.dram_tensor("chosen_d", [images * E, S], F32, kind="Internal").ap()
    patches_d = [nc.dram_tensor(f"patches_{parity}", [PATCHES, GROUPS * 4 * CG], F32, kind="Internal").ap()
                 for parity in ("even", "odd")]
    expert_d = nc.dram_tensor("expert_d", [E, images, C], F32, kind="Internal").ap()
    first_layer_and_attention(nc, io, x2_d, xln2_d, logits_d, patches_d, images)
    route_and_experts(nc, io, xln2_d, logits_d, chosen_d, expert_d, images)
    combine(nc, io, x2_d, chosen_d, expert_d, out, images)


def kernel(**inputs):
    import numpy as np
    import concourse.bacc as bacc
    from concourse.bass_utils import run_bass_kernel_spmd as run

    images = inputs["x"].shape[0]
    arrays = layout(inputs)
    nc = bacc.Bacc("TRN2", target_bir_lowering=False, num_devices=1)
    io = {k: nc.dram_tensor(f"in_{k}", a.shape, F32, kind="ExternalInput").ap() for k, a in arrays.items()}
    out = nc.dram_tensor("out_x", (images * S, C), F32, kind="ExternalOutput").ap()
    program(nc, io, out, images)
    r = run(nc, [{f"in_{k}": a for k, a in arrays.items()}], core_ids=[0])
    return np.asarray(r.results[0]["out_x"]).reshape(inputs["x"].shape)
```

```python
import concourse.bass as bass
from concourse import mybir
from contextlib import ExitStack

F32 = mybir.dt.float32
I32 = mybir.dt.int32
U32 = mybir.dt.uint32
ALU = mybir.AluOpType
ACT = mybir.ActivationFunctionType
AX_X = mybir.AxisListType.X

P = 128
C = 128
H = W = 56
S = H * W
GROUPS, CG, TAPS = 4, 32, 9
HP = H + 2
PATCHES = HP * HP
NPATCH = (PATCHES + P - 1) // P
SUB = 64
NSUB = S // SUB
SAMPLES = GROUPS // 2 * TAPS
BAND_ROWS = 8
BAND = BAND_ROWS * W
NBAND = H // BAND_ROWS
BAND_SUBS = BAND // SUB
PARAMS = GROUPS // 2 * TAPS * 3
NBLK = (S + P - 1) // P
A = 16
ROWS8 = P // A
CHUNK = 1024
E = 64
K_TOP = 8
HID = 512
EPS = 1e-5
GATHER_SLOTS = 5
X1_SLOTS = 10
TANH_SLOTS = 5
FLOOR_MAGIC = 8388608.0
RSQRT_MAGIC = 1597463007.0


def blk_rows(k):
    return min(P, S - k * P)


def patch_rows(i):
    return min(P, PATCHES - i * P)


def chunks_of(k):
    tiles = k + 1
    n = -(-tiles * P // CHUNK)
    cuts = [tiles * i // n for i in range(n + 1)]
    return [list(range(cuts[i], cuts[i + 1])) for i in range(n)]


def chunk_width(tiles):
    return sum(blk_rows(j) for j in tiles)


EARLY = 5


def key_column(odd, k):
    return (EARLY * P + S) - k * P - blk_rows(k) if odd else k * P


def value_place(odd, k):
    return NBLK + EARLY - 1 - k if odd else k


def x1_place(odd, k):
    return ((NBLK if odd else 0) + k) % X1_SLOTS


def column_in_chunk(odd, tiles, j):
    return key_column(odd, j) - key_column(odd, tiles[-1] if odd else tiles[0])


CHUNK_INDEX = {}
UNIT_INDEX = {}
QUAD_INDEX = {}
for _k in range(NBLK):
    for _c, _tiles in enumerate(chunks_of(_k)):
        CHUNK_INDEX[_k, _c] = len(CHUNK_INDEX)
        for _s in range(blk_rows(_k) // ROWS8):
            UNIT_INDEX[_k, _c, _s] = len(UNIT_INDEX)
        for _p in range(-(-len(_tiles) // 4)):
            QUAD_INDEX[_k, _c, _p] = len(QUAD_INDEX)
CHUNKS, UNITS, QUADS = len(CHUNK_INDEX), len(UNIT_INDEX), len(QUAD_INDEX)


def gather_slot(t):
    return t % GATHER_SLOTS


SLOT_USES = [sum(gather_slot(t) == b for t in range(NSUB)) for b in range(GATHER_SLOTS)]


def slot_use(t):
    return sum(gather_slot(u) == gather_slot(t) for u in range(t))


def last_user(t):
    for u in range(t - 1, t - NSUB - 1, -1):
        if gather_slot(u % NSUB) == gather_slot(t):
            return u


DUE_BLOCKS = 24.6
CHAIN_URGENT = 2
SAMPLE_URGENT = 1
READY = 1.3
SHARE = (1.75, 8, 33)
CHAIN_BEGIN = 0.8
HANDOFF = 0.1
DMA_US = 2.3
TABLE_US = 1.3
GATHER_US = 1.04
CHAIN = ("turn", "mix", "turn_mid", "hidden", "mlp_out", "turn_norm", "keys")
CHAIN_AT = (.0, .1, .27, .37, .5, .75, .85)
SIDE = ("image_in", "project_in", "patches", "conv", "offsets", "route", "logits")
SIDE_READER = {"conv": "act"}
LASTS = {
    ("pe", "image_in"): .6, ("pe", "project_in"): 1.3, ("pe", "patches"): .6, ("pe", "conv"): 11.5, ("pe", "offsets"): 2.5,
    ("pe", "turn"): .45, ("pe", "mix"): 1.5, ("pe", "turn_mid"): .45, ("pe", "hidden"): 2.1, ("pe", "mlp_out"): 1.4,
    ("pe", "turn_norm"): .45, ("pe", "keys"): 1.5, ("pe", "route"): .25, ("pe", "logits"): .3,
    ("dve", "image_in"): .7, ("dve", "project_in"): .7, ("dve", "patches"): .8, ("dve", "offsets"): 3.5, ("dve", "weights"): 2.8,
    ("dve", "sample"): 5.2, ("dve", "turn"): .4, ("dve", "mix"): 3.9, ("dve", "turn_mid"): .4, ("dve", "mlp_out"): 7.2,
    ("dve", "turn_norm"): .4, ("dve", "keys"): .6, ("dve", "mask"): .4, ("dve", "finish"): 4.5, ("dve", "route"): .4, ("dve", "logits"): .4,
    ("act", "conv"): .6, ("act", "offsets"): .3, ("act", "hidden"): .7,
}


def lasts(engine, step):
    what = step[0]
    if (engine, what) in LASTS:
        return LASTS[engine, what]
    if engine == "sp":
        return .1
    if engine == "pool":
        return SAMPLES * GATHER_US
    tiles = chunks_of(step[1])[step[2]]
    w = chunk_width(tiles)
    if what == "unit":
        return w * .00066 + .05 if engine == "pe" else w * .00079 + .19
    if what == "exp":
        return w * .00079 + .25
    q = step[3]
    turned, summed = len(tiles[4 * q:4 * q + 4]), len(tiles[4 * q - 4:4 * q]) if q else 0
    return .13 * turned + .33 * summed + .05 if engine == "pe" else .2 * turned + .2


def due_times():
    due = {}
    for g in range(NBAND):
        due["image_in", g] = g + .2 - DUE_BLOCKS
        due["project_in", g] = g + .7 - DUE_BLOCKS
        last = (g + 1) * BAND_SUBS / 2 - .2 - DUE_BLOCKS if g < NBAND - 1 else -.75
        due["conv", g], due["offsets", g], due["weights", g] = last, last + .2, last + .5
    for t in range(NPATCH):
        due["patches", t] = 7 + t * .26 - DUE_BLOCKS
    free = 3.0
    for k in range(NBLK):
        due["x_in", k] = k - .02
        begin, pace = k + CHAIN_BEGIN, 1
        due["sample", 2 * k] = k - SAMPLE_URGENT
        if 2 * k + 1 < NSUB:
            due["sample", 2 * k + 1] = k + .5 - SAMPLE_URGENT
        else:
            begin, pace = k + .46, .75
        for name, at in zip(CHAIN, CHAIN_AT):
            due[name, k] = begin + pace * at - CHAIN_URGENT
        begin = max(free, begin + READY)
        span = max(.4, (SHARE[0] * (k + 1) + SHARE[1]) / SHARE[2] * blk_rows(k) / P)
        units = [u for u in UNIT_INDEX if u[0] == k]
        d = span / len(units)
        for i, u in enumerate(units):
            due["unit", *u] = begin + d * i
        for c, tiles in enumerate(chunks_of(k)):
            end = begin + d * (blk_rows(k) // ROWS8) * (c + 1)
            due["exp", k, c] = end
            due["mask", k] = end + .02
            for q in range(-(-len(tiles) // 4) + 1):
                due["values", k, c, q] = end + .05 + .05 * q
        due["finish", k], due["route", k], due["logits", k] = end + .2, end + .3, end + .4
        free = begin + span
    return due


def needs():
    out = {}

    def at(age, engine, what, *place):
        return age, engine, (what, *place)

    def before(engine, what, i, count, ring=1):
        return at(0, engine, what, i - ring) if i >= ring else at(1, engine, what, count - 1)

    quads = list(QUAD_INDEX)
    units = list(UNIT_INDEX)
    chunks = list(CHUNK_INDEX)
    for g in range(NBAND):
        used = at(1, "dve", "sample", (g + 1) * BAND_SUBS - 1)
        out["sp", ("image_in", g)] = [before("pe", "image_in", g, NBAND, 2), at(1, "dve", "sample", 2 * g)]
        out["pe", ("image_in", g)] = [at(0, "sp", "image_in", g), at(1, "pe", "conv", NBAND - 1)]
        out["dve", ("image_in", g)] = [at(0, "pe", "image_in", g)]
        out["pe", ("project_in", g)] = [at(0, "dve", "image_in", g), at(1, "pe", "patches", NPATCH - 1)]
        out["dve", ("project_in", g)] = [at(0, "pe", "project_in", g)]
        out["pe", ("conv", g)] = [at(0, "dve", "image_in", min(g + 1, NBAND - 1)), used,
                                  before("pe", "offsets", g, NBAND)]
        out["act", ("conv", g)] = [at(0, "pe", "conv", g)]
        out["pe", ("offsets", g)] = [at(0, "act", "conv", g), before("dve", "weights", g, NBAND)]
        out["dve", ("offsets", g)] = [at(0, "pe", "offsets", g)]
        out["act", ("offsets", g)] = [at(0, "dve", "offsets", g)]
        out["dve", ("weights", g)] = [at(0, "act", "offsets", g)]
    for t in range(NPATCH):
        band = min(NBAND - 1, ((t * P + P + HP) // HP - 1) // BAND_ROWS)
        out["pe", ("patches", t)] = [at(0, "dve", "project_in", band)]
        out["dve", ("patches", t)] = [at(0, "pe", "patches", t), before("sp", "patches", t, NPATCH, 2)]
        out["sp", ("patches", t)] = [at(0, "dve", "patches", t), at(2, "dve", "sample", NSUB - 1)]
    for t in range(NSUB):
        last = last_user(t)
        out["pool", ("sample", t)] = [at(0, "dve", "offsets", t // BAND_SUBS), at(0, "sp", "patches", NPATCH - 1),
                                      at(0, "sp", "patches", NPATCH - 2),
                                      at(int(last < 0), "dve", "sample", last % NSUB)]
        out["dve", ("sample", t)] = [at(0, "pool", "sample", t), at(0, "dve", "weights", t // BAND_SUBS),
                                     before("pe", "turn", t // 2, NBLK, 2)]
    for k in range(NBLK):
        last = (k, len(chunks_of(k)) - 1)
        end = at(0, "pe", "values", *last, -(-len(chunks_of(k)[-1]) // 4))
        old = k if k < EARLY else NBLK - 1
        out["sp", ("x_in", k)] = [before("dve", "mix", k, NBLK, 2), before("dve", "sample", k, NBLK, 2)]
        out["pe", ("turn", k)] = [at(0, "dve", "sample", min(2 * k + 1, NSUB - 1)), before("dve", "keys", k, NBLK)]
        out["dve", ("turn", k)] = [at(0, "pe", "turn", k)]
        out["pe", ("mix", k)] = [at(0, "dve", "turn", k)]
        out["dve", ("mix", k)] = [at(0, "pe", "mix", k), at(0, "sp", "x_in", k)]
        out["pe", ("turn_mid", k)] = [at(0, "dve", "mix", k)]
        out["dve", ("turn_mid", k)] = [at(0, "pe", "turn_mid", k)]
        out["pe", ("hidden", k)] = [at(0, "dve", "turn_mid", k)]
        out["act", ("hidden", k)] = [at(0, "pe", "hidden", k)]
        out["pe", ("mlp_out", k)] = [at(0, "act", "hidden", k)]
        out["dve", ("mlp_out", k)] = [at(0, "pe", "mlp_out", k), at(int(k < X1_SLOTS), "dve", "finish", (k - X1_SLOTS) % NBLK),
                                      at(1, "pe", "values", old, len(chunks_of(old)) - 1, -(-len(chunks_of(old)[-1]) // 4))]
        out["pe", ("turn_norm", k)] = [at(0, "dve", "mlp_out", k)]
        out["dve", ("turn_norm", k)] = [at(0, "pe", "turn_norm", k)]
        out["pe", ("keys", k)] = [at(0, "dve", "turn_norm", k)]
        out["dve", ("keys", k)] = [at(0, "pe", "keys", k),
                                   at(1, "act", "unit", old, len(chunks_of(old)) - 1, blk_rows(old) // ROWS8 - 1)]
        out["dve", ("mask", k)] = [at(0, "act", "exp", *last)]
        out["dve", ("finish", k)] = [end, before("sp", "route", k, NBLK, 2), before("sp", "logits", k, NBLK, 2),
                                     before("pe", "route", k, NBLK)]
        out["sp", ("route", k)] = [at(0, "dve", "finish", k)]
        out["pe", ("route", k)] = [at(0, "dve", "finish", k), before("pe", "logits", k, NBLK)]
        out["dve", ("route", k)] = [at(0, "pe", "route", k)]
        out["pe", ("logits", k)] = [at(0, "dve", "route", k)]
        out["dve", ("logits", k)] = [at(0, "pe", "logits", k)]
        out["sp", ("logits", k)] = [at(0, "dve", "logits", k), at(0, "sp", "route", k)]
    for i, u in enumerate(units):
        ci = CHUNK_INDEX[u[:2]]
        ring = units[i - TANH_SLOTS if i >= TANH_SLOTS or UNITS % TANH_SLOTS == 0 else -1]
        out["act", ("unit", *u)] = [at(0, "dve", "keys", u[0]), at(int(i < TANH_SLOTS), "pe", "unit", *ring)]
        out["pe", ("unit", *u)] = [at(0, "act", "unit", *u), at(int(ci < 2), "act", "exp", *chunks[ci - 2])]
    for i, (k, c) in enumerate(chunks):
        old = chunks[i - 2]
        out["act", ("exp", k, c)] = [at(0, "pe", "unit", k, c, blk_rows(k) // ROWS8 - 1),
                                     at(int(i < 2), "pe", "values", *old, -(-len(chunks_of(old[0])[old[1]]) // 4) - 1)]
        n = -(-len(chunks_of(k)[c]) // 4)
        for q in range(n + 1):
            need = [at(0, "act", "exp", k, c)]
            if c == len(chunks_of(k)) - 1:
                need.append(at(0, "dve", "mask", k))
            if q:
                need.append(at(0, "dve", "values", k, c, q - 1))
            if (c, q) == (0, 1):
                need.append(before("dve", "finish", k, NBLK))
            if q < n:
                pi = QUAD_INDEX[k, c, q]
                need.append(at(int(pi < 1), "dve", "values", *quads[pi - 1]))
                ok, oc, oq = quads[pi - 2 if pi >= 2 or QUADS % 2 == 0 else -1]
                out["dve", ("values", k, c, q)] = [at(0, "pe", "values", k, c, q),
                                                   at(int(pi < 2), "pe", "values", ok, oc, oq + 1)]
            out["pe", ("values", k, c, q)] = need
    kinds = {}
    for engine, step in list(out):
        if (engine, step[0]) in kinds:
            out[engine, step].append((0, engine, kinds[engine, step[0]]))
        kinds[engine, step[0]] = step
    for engine, step in list(out):
        if kinds[engine, step[0]] != step and all(e != engine or s[0] != step[0] for _, e, s in out[engine, step]):
            out[engine, step].append((1, engine, kinds[engine, step[0]]))
    return out


def list_schedule(images=6):
    due, need = due_times(), needs()
    waiting, users, ready = {}, {}, {e: [] for e in ("pe", "dve", "act", "sp", "pool")}
    times = {}
    met = {}

    def add(n, engine, step):
        ready[engine].append((n * DUE_BLOCKS + due[step], n, step))

    for n in range(images):
        for (engine, step), before in need.items():
            known = {(n - age, e, s) for age, e, s in before if n >= age}
            waiting[n, engine, step] = len(known)
            for x in known:
                users.setdefault(x, []).append((n, engine, step))
            if not known:
                add(n, engine, step)
    table = False
    side_free = True
    busy = {e: False for e in ready}
    events = []
    now = 0.0
    serial = 0
    while True:
        for e in ready:
            if busy[e] or not ready[e]:
                continue
            able = [x for x in ready[e] if side_free or e != "pe" or x[2][0] not in SIDE]
            if not able:
                continue
            choice = min(able)
            ready[e].remove(choice)
            _, n, step = choice
            if e == "pe" and step[0] in SIDE:
                side_free = False
            times[n, e, step] = now
            busy[e] = True
            end = now + lasts(e, step)
            if e == "act" and step[0] != "unit" and table != (step[0] in ("conv", "hidden")):
                table = not table
                end += TABLE_US
            events.append((end, serial, "free", e, n, step))
            events.append((end + (DMA_US if e in ("sp", "pool") else HANDOFF), serial + 1, "done", e, n, step))
            serial += 2
        if not events:
            break
        event = min(events)
        events.remove(event)
        now, _, what, e, n, step = event
        if what == "free":
            busy[e] = False
        elif step[0] in SIDE and e == SIDE_READER.get(step[0], "dve"):
            side_free = True
        for x in users.get((n, e, step), ()):
            if (x[1] == e) == (what == "free"):
                waiting[x] -= 1
                if not waiting[x]:
                    add(*x)
    if len(times) < images * len(need):
        raise ValueError("the steps wait for each other")
    m = images - 3
    start = times[m, "dve", ("sample", 0)]
    period = times[m + 1, "dve", ("sample", 0)] - start
    return {(e, s): times[m, e, s] - start for e, s in need}, period


def order_of(engine, schedule):
    times, period = schedule
    out = []
    for (e, step), t in times.items():
        if e == engine:
            age = int(t // period)
            if not -1 <= age <= 1:
                raise ValueError("a step is too far from its image")
            out.append((t - age * period, age, step))
    out.sort()
    return [(age, step) for _, age, step in out]


class Line:

    def __init__(self, sem, per_image, step=1):
        self.sem, self.per_image, self.step = sem, per_image, step

    @property
    def lead(self):
        return self.per_image * self.step

    def after(self, image, i):
        return image * self.lead + (self.lead + (i + 1) * self.step)

    def free(self, image, i, ring):
        return self.after(image, i - ring if i >= ring or self.per_image % ring == 0 else -1)


def first_layer_and_attention(nc, io, x2_d, xln2_d, logits_d, patches_d, images):
    with ExitStack() as ctx:
        def sb(name, shape, dt=F32):
            return ctx.enter_context(nc.sbuf_tensor(name, shape, dt))

        def ps(name, shape):
            return ctx.enter_context(nc.psum_tensor(name, shape, F32))

        def sem(name):
            return ctx.enter_context(nc.semaphore(name))

        ident = sb("ident", [P, P])
        earlier = sb("earlier", [P, P])
        score_place = sb("score_place", [P, 4, 32])
        score_w = sb("score_w", [P, 4, 32])
        grid = sb("grid", [P, BAND_SUBS, 2 * SAMPLES])
        base_index = sb("base_index", [P, SAMPLES])
        chan = sb("chan", [P, 6])
        dw = sb("dw", [P, TAPS])
        taps = sb("taps", [P, TAPS, C])
        bn = sb("bn", [P, 2])
        w_in = sb("w_in", [C, C])
        w_par = sb("w_par", [C, 2, PARAMS])
        b_par = sb("b_par", [P, PARAMS])
        w_out = sb("w_out", [P, 2, C])
        w_fc1 = sb("w_fc1", [C, HID])
        w_fc2 = sb("w_fc2", [P, HID // P, C])
        rows = sb("rows", [1, HID + 2 * C])
        ones = sb("ones", [1, P])
        affine = sb("affine", [P, 6, C])
        w_key = sb("w_key", [C, ROWS8, A])
        w_q = sb("w_q", [C, A])
        w_query = sb("w_query", [C, ROWS8, ROWS8, A])
        tiny = sb("tiny", [P, 3])
        gate_w = sb("gate_w", [C, E])
        gate_b = sb("gate_b", [E, 1])
        x_band = sb("x_band", [112, 2, 4, C])
        x_pad = sb("x_pad", [C, HP, HP])
        xp_flat = sb("xp_flat", [C, PATCHES + HP + 2])
        patch = sb("patch", [P, 2, GROUPS, 4, CG])
        h_band = sb("h_band", [C, BAND])
        xy = sb("xy", [P, BAND_SUBS, SAMPLES, 2])
        cell = sb("cell", [P, BAND_SUBS, SAMPLES, 2])
        flat = sb("flat", [P, BAND_SUBS, SAMPLES])
        mask = sb("mask", [P, BAND_SUBS, SAMPLES])
        upper = sb("upper", [P, BAND_SUBS, SAMPLES])
        lower = sb("lower", [P, BAND_SUBS, SAMPLES])
        stat = sb("stat", [P, BAND_SUBS * 2])
        index = sb("index", [P, NBAND, BAND_SUBS * SAMPLES], I32)
        corner_w = sb("corner_w", [P, NBAND, BAND_SUBS, SAMPLES * 4])
        gathered = sb("gathered", [P, GATHER_SLOTS, SAMPLES * 4 * CG])
        y = sb("y", [P, 2, 2, 2 * CG])
        yT = sb("yT", [P, P])
        x_tok = sb("x_tok", [P, 2, C])
        mid = sb("mid", [P, C])
        midT = sb("midT", [C, P])
        hid = sb("hid", [P, HID // P, P])
        x1 = sb("x1", [P, X1_SLOTS, C])
        ln_a = sb("ln_a", [P, C])
        ln_b = sb("ln_b", [P, C])
        lnT = sb("lnT", [C, P])
        bst = sb("bst", [P, 6])
        mv = sb("mv", [P, 2])
        var = sb("var", [P, 1])
        rstd = sb("rstd", [P, 1])
        newton = sb("newton", [P, 2])
        key_rep = sb("key_rep", [P, EARLY * P + S])
        query = sb("query", [P, NBLK * A])
        values = sb("values", [P, NBLK + EARLY, C + 1])
        tanh = sb("tanh", [P, TANH_SLOTS, CHUNK])
        expo = sb("expo", [P, 2, CHUNK])
        expoT = sb("expoT", [P, 2, 4, P])
        den = sb("den", [P, 2])
        x2 = sb("x2", [P, 2, C])
        xln2 = sb("xln2", [P, 2, C])
        xln2T = sb("xln2T", [C, P])
        logit = sb("logit", [E, 2, P])

        score_ps = ps("score_ps", [P, 2, CHUNK])
        turn_ps = ps("turn_ps", [P, 4, P])
        value_ps = ps("value_ps", [P, 512])
        chain_ps = ps("chain_ps", [P, 512])
        side_ps = ps("side_ps", [P, 512])

        consts_in = sem("consts_in")
        consts_ready = sem("consts_ready")
        prologue_go = sem("prologue_go")
        pool_step = sem("pool_step")
        pe_step = sem("pe_step")
        x_band_in = [Line(sem(f"x_band_in{i}"), (NBAND + 1 - i) // 2, 16) for i in range(2)]
        patches_out = [Line(sem(f"patches_out{i}"), (NPATCH + 1 - i) // 2, 16) for i in range(2)]
        x_tok_in = [Line(sem(f"x_tok_in{i}"), (NBLK + 1 - i) // 2, 16) for i in range(2)]
        block_out = [Line(sem(f"block_out{i}"), (NBLK + 1 - i) // 2, 48) for i in range(2)]
        gather_done = [sem(f"gather_done{i}") for i in range(GATHER_SLOTS)]

        def line(name, per_image):
            return Line(sem(name), per_image)

        band_turned = line("band_turned", NBAND)
        band_copied = line("band_copied", NBAND)
        in_projected = line("in_projected", NBAND)
        in_copied = line("in_copied", NBAND)
        patch_turned = line("patch_turned", NPATCH)
        patch_ready = line("patch_ready", NPATCH)
        conv_done = line("conv_done", NBAND)
        h_ready = line("h_ready", NBAND)
        params_done = line("params_done", NBAND)
        index_ready = line("index_ready", NBAND)
        mask_shifted = line("mask_shifted", NBAND)
        mask_exp = line("mask_exp", NBAND)
        sampled = line("sampled", NSUB)
        y_turned = line("y_turned", NBLK)
        y_copied = line("y_copied", NBLK)
        mixed = line("mixed", NBLK)
        mid_ready = line("mid_ready", NBLK)
        mid_turned = line("mid_turned", NBLK)
        mid_copied = line("mid_copied", NBLK)
        hid_done = line("hid_done", NBLK)
        gelu_done = line("gelu_done", NBLK)
        mlp_done = line("mlp_done", NBLK)
        norm_ready = line("norm_ready", NBLK)
        norm_turned = line("norm_turned", NBLK)
        norm_copied = line("norm_copied", NBLK)
        keys_done = line("keys_done", NBLK)
        keys_copied = line("keys_copied", NBLK)
        tanh_done = line("tanh_done", UNITS)
        scored = line("scored", UNITS)
        exp_done = line("exp_done", CHUNKS)
        masked = line("masked", NBLK)
        exp_turned = line("exp_turned", QUADS)
        exp_copied = line("exp_copied", QUADS)
        quad_used = line("quad_used", QUADS)
        x2_ready = line("x2_ready", NBLK)
        ln2_ready = line("ln2_ready", NBLK)
        ln2_turned = line("ln2_turned", NBLK)
        ln2_copied = line("ln2_copied", NBLK)
        logits_done = line("logits_done", NBLK)
        logits_copied = line("logits_copied", NBLK)

        side_read = sem("side_read")

        schedule = list_schedule()
        side_uses_of = {age: sum(a == age and step[0] in SIDE and step[0] != "conv"
                                 for a, step in order_of("pe", schedule)) for age in (-1, 0, 1)}
        last_conv_of_period = [(age, step[1]) for age, step in order_of("pe", schedule) if step[0] == "conv"][-1]

        block = ctx.enter_context(nc.Block())

        def walk(engine, name, task, begin=lambda n: None):
            def period(n, odd, ages=(-1, 0, 1)):
                begin(n)
                for age, step in order_of(name, schedule):
                    if age in ages:
                        task(n - age, odd if age == 0 else not odd, step)

            period(-1, True, (-1,))
            period(0, False, (-1, 0))
            if images > 2:
                with engine.Fori(0, images // 2 - 1) as pair:
                    period(pair * 2 + 1, True)
                    period(pair * 2 + 2, False)
            period(images - 1, True, (0, 1))
            period(images, False, (1,))

        @block.sync
        def _(sp):
            names = ["ident", "earlier", "score_place", "grid", "base_index", "chan", "dw", "w_in", "w_par",
                     "b_par", "w_out", "w_fc1", "w_fc2", "rows", "affine", "w_key", "w_q", "tiny", "gate_w", "gate_b"]
            tiles = dict(ident=ident, earlier=earlier, score_place=score_place, grid=grid, base_index=base_index,
                         chan=chan, dw=dw, w_in=w_in, w_par=w_par, b_par=b_par, w_out=w_out, w_fc1=w_fc1,
                         w_fc2=w_fc2, rows=rows, affine=affine, w_key=w_key, w_q=w_q, tiny=tiny, gate_w=gate_w, gate_b=gate_b)
            for name in names:
                sp.dma_start(tiles[name][:], io[name]).then_inc(consts_in, 16)
            for ln in (*x_band_in, *patches_out, *x_tok_in, *block_out):
                nc.sync.sem_inc(ln.sem, ln.lead)

            def task(n, odd, name):
                what, i = name[:2]
                b = i % 2
                if what == "image_in":
                    sp.wait_ge(band_turned.sem, band_turned.free(n, i, 2))
                    sp.dma_start(x_band[:, b], io["x"][bass.ds(n * S + i * BAND, BAND), :]
                                 .rearrange("(q p) c -> p q c", p=112)).then_inc(x_band_in[b].sem, 16)
                elif what == "patches":
                    sp.wait_ge(patch_ready.sem, patch_ready.after(n, i))
                    if i < 2 and not (isinstance(n, int) and n == 0):
                        sp.wait_ge(sampled.sem, sampled.after(n - 1, -1))
                    sp.dma_start(patches_d[int(odd)][i * P:i * P + patch_rows(i), :],
                                 patch[:patch_rows(i), b].rearrange("p g k c -> p (g k c)")).then_inc(patches_out[b].sem, 16)
                elif what == "x_in":
                    sp.wait_ge(mid_ready.sem, mid_ready.free(n, i, 2))
                    sp.dma_start(x_tok[:blk_rows(i), b], io["x"][bass.ds(n * S + i * P, blk_rows(i)), :])\
                        .then_inc(x_tok_in[b].sem, 16)
                elif what == "route":
                    r = blk_rows(i)
                    sp.wait_ge(ln2_ready.sem, ln2_ready.after(n, i))
                    sp.dma_start(x2_d[bass.ds(n * S + i * P, r), :], x2[:r, b]).then_inc(block_out[b].sem, 16)
                    sp.dma_start(xln2_d[bass.ds(n * S + i * P, r), :], xln2[:r, b]).then_inc(block_out[b].sem, 16)
                elif what == "logits":
                    r = blk_rows(i)
                    sp.wait_ge(logits_copied.sem, logits_copied.after(n, i))
                    sp.dma_start(logits_d[bass.ds(n * E, E), i * P:i * P + r], logit[:, b, :r])\
                        .then_inc(block_out[b].sem, 16)

            walk(sp, "sp", task)
            for ln in block_out:
                sp.wait_ge(ln.sem, ln.after(images - 1, ln.per_image - 1))
            for ln in patches_out:
                sp.wait_ge(ln.sem, ln.after(images - 1, ln.per_image - 1))

        @block.gpsimd
        def _(pool):
            def gathers(n, odd):
                for ln in patches_out:
                    pool.wait_ge(ln.sem, ln.after(n, ln.per_image - 1))
                    nc.gpsimd.sem_inc(pool_step, 1)
                for t in range(NSUB):
                    g, tt = divmod(t, BAND_SUBS)
                    b = gather_slot(t)
                    if tt == 0:
                        pool.wait_ge(index_ready.sem, index_ready.after(n, g))
                        nc.gpsimd.sem_inc(pool_step, 1)
                    pool.wait_ge(sampled.sem, sampled.after(n, last_user(t)))
                    nc.gpsimd.sem_inc(pool_step, 1)
                    for j in range(SAMPLES):
                        at = tt * SAMPLES + j
                        pool.indirect_dma_start(
                            gathered[:, b, j * 4 * CG:(j + 1) * 4 * CG], None, patches_flat[int(odd)],
                            bass.IndirectOffsetOnAxis(ap=index[:, g, at:at + 1].bitcast(U32), axis=0),
                        ).then_inc(gather_done[b], 16)

            patches_flat = [d.rearrange("n (g k) -> (n g) k", g=GROUPS) for d in patches_d]
            gathers(0, False)
            if images > 2:
                with pool.Fori(1, images - 1, 2) as n:
                    gathers(n, True)
                    gathers(n + 1, False)
            gathers(images - 1, True)

        @block.vector
        def _(dve):
            v = nc.vector

            def settle():
                return v.drain()

            for ln in (band_copied, in_copied, patch_ready, index_ready, mask_shifted, sampled, y_copied, mid_ready,
                       mid_copied, norm_ready, norm_copied, keys_copied, masked, exp_copied, x2_ready, ln2_ready,
                       ln2_copied, logits_copied):
                v.sem_inc(ln.sem, ln.lead)
            v.memset(x_pad[:], 0.0)
            v.memset(xp_flat[:], 0.0)
            v.memset(w_query[:], 0.0)
            v.memset(ones[:], 1.0)
            v.memset(y[:], 0.0)
            v.memset(values[:, :, C:C + 1], 1.0)
            settle()
            dve.wait_ge(consts_in, 16 * 20)
            for t in range(TAPS):
                v.tensor_scalar(taps[:, t], ident[:], dw[:, t:t + 1], None, ALU.mult)
            for i in range(ROWS8):
                v.tensor_copy(w_query[:, i, i], w_q[:])
            v.tensor_scalar(score_w[:], score_place[:], tiny[:, 1:2], None, ALU.mult)
            v.tensor_tensor(grid[:], grid[:], b_par[:, None, 0:2 * SAMPLES].to_broadcast([P, BAND_SUBS, 2 * SAMPLES]),
                            ALU.add)
            for s in (0, 3):
                v.tensor_tensor(affine[:, s], affine[:, s], affine[:, s + 2], ALU.mult)
                v.tensor_tensor(affine[:, s + 1], affine[:, s + 1], affine[:, s + 2], ALU.mult)
            v.tensor_tensor(bn[:, 1:2], chan[:, 1:2], chan[:, 4:5], ALU.subtract)
            settle()

            def rsqrt(src, r):
                v.tensor_scalar(var[:r], src, EPS, None, ALU.add)
                v.tensor_scalar(newton[:r, 0:1], src, EPS, -0.5, ALU.add, ALU.mult)
                settle()
                v.tensor_scalar(rstd[:r].bitcast(I32), var[:r].bitcast(I32), -0.5, RSQRT_MAGIC, ALU.mult, ALU.add)
                settle()
                for _ in range(3):
                    v.tensor_scalar(newton[:r, 1:2], rstd[:r], rstd[:r], newton[:r, 0:1], ALU.mult, ALU.mult)
                    settle()
                    v.tensor_scalar(rstd[:r], newton[:r, 1:2], 1.5, rstd[:r], ALU.add, ALU.mult)
                    settle()

            def moments(src, r):
                v.bn_stats(bst[:r], src)
                settle()
                v.bn_aggr(mv[:r], bst[:r])
                settle()
                rsqrt(mv[:r, 1:2], r)

            rsqrt(chan[:, 5:6], P)
            v.tensor_tensor(bn[:, 0:1], rstd[:], chan[:, 2:3], ALU.mult)
            settle()
            v.scalar_tensor_tensor(bn[:, 1:2], bn[:, 1:2], bn[:, 0:1], chan[:, 3:4], ALU.mult, ALU.add)
            settle().then_inc(consts_ready, 1)

            def wait(ln, image, i):
                dve.wait_ge(ln.sem, ln.after(image, i))

            def add_norm(src, out, residual, s, r):
                moments(src, r)
                v.scalar_tensor_tensor(ln_a[:r], src, mv[:r, 0:1], affine[:r, s], ALU.subtract, ALU.mult)
                v.tensor_tensor(ln_b[:r], residual, affine[:r, s + 1], ALU.add)
                settle()

            def task(n, odd, name):
                what, i = name[:2]
                b = i % 2
                if what == "image_in":
                    rs = slice(1 + i * BAND_ROWS, 1 + (i + 1) * BAND_ROWS)
                    wait(band_turned, n, i)
                    wait(conv_done, n, -1)
                    v.tensor_copy(x_pad[:, rs, 1:W + 1], side_ps[:, :BAND].rearrange("p (a b) -> p a b", b=W))\
                        .then_inc(band_copied.sem, 1)
                    settle().then_inc(side_read, 1)
                elif what == "project_in":
                    rs = slice(1 + i * BAND_ROWS, 1 + (i + 1) * BAND_ROWS)
                    wait(in_projected, n, i)
                    wait(patch_turned, n, -1)
                    v.tensor_scalar(xp_flat[:, :PATCHES].rearrange("p (a b) -> p a b", b=HP)[:, rs, 1:W + 1], side_ps[:, :BAND].rearrange("p (a b) -> p a b", b=W),
                                    chan[:, 0:1], None, ALU.add)\
                        .then_inc(in_copied.sem, 1)
                    settle().then_inc(side_read, 1)
                elif what == "patches":
                    wait(patch_turned, n, i)
                    dve.wait_ge(patches_out[b].sem, patches_out[b].after(n, i // 2 - 1))
                    v.tensor_copy(patch[:patch_rows(i), b].rearrange("p g k c -> p k g c"),
                                  side_ps[:patch_rows(i)].rearrange("p (k g c) -> p k g c", k=4, g=GROUPS))\
                        .then_inc(patch_ready.sem, 1)
                    settle().then_inc(side_read, 1)
                elif what == "offsets":
                    wait(params_done, n, i)
                    par = side_ps[:, :BAND_SUBS * PARAMS].rearrange("p (t c) -> p t c", c=PARAMS)
                    xyf = xy[:].rearrange("p t s a -> p t (s a)")
                    v.tensor_tensor(xyf, par[:, :, :2 * SAMPLES], grid[:], ALU.add)
                    v.tensor_tensor(mask[:], par[:, :, 2 * SAMPLES:],
                                    b_par[:, None, 2 * SAMPLES:].to_broadcast([P, BAND_SUBS, SAMPLES]), ALU.add)
                    settle().then_inc(side_read, 1)
                    mask9 = mask[:].rearrange("p t (g s) -> p (t g) s", s=TAPS)
                    v.tensor_reduce(stat[:], mask9, AX_X, ALU.max)
                    if i:
                        v.tensor_scalar(xy[:, :, :, 1], xy[:, :, :, 1], float(BAND_ROWS * i), None, ALU.add)
                    settle()
                    v.tensor_tensor(mask9, mask9, stat[:].unsqueeze(2).to_broadcast([P, BAND_SUBS * 2, TAPS]),
                                    ALU.subtract)
                    v.tensor_scalar(xy[:], xy[:], float(HP - 1), 0.0, ALU.min, ALU.max)
                    settle().then_inc(mask_shifted.sem, 1)
                    v.tensor_scalar(cell[:], xy[:], FLOOR_MAGIC, FLOOR_MAGIC, ALU.add, ALU.subtract)
                    settle()
                    above = corner_w[:, i, :, :2 * SAMPLES].rearrange("p t (s a) -> p t s a", a=2)
                    v.tensor_tensor(above, cell[:], xy[:], ALU.is_gt)
                    settle()
                    v.tensor_tensor(cell[:], cell[:], above, ALU.subtract)
                    settle()
                    v.tensor_tensor(xy[:], xy[:], cell[:], ALU.subtract)
                    v.scalar_tensor_tensor(flat[:], cell[:, :, :, 1], float(HP), cell[:, :, :, 0], ALU.mult, ALU.add)
                    settle()
                    v.scalar_tensor_tensor(index[:, i].rearrange("p (t s) -> p t s", s=SAMPLES), flat[:],
                                           float(GROUPS), base_index[:, None, :].to_broadcast([P, BAND_SUBS, SAMPLES]),
                                           ALU.mult, ALU.add)
                    settle().then_inc(index_ready.sem, 1)
                elif what == "weights":
                    wait(mask_exp, n, i)
                    mask9 = mask[:].rearrange("p t (g s) -> p (t g) s", s=TAPS)
                    v.tensor_reduce(stat[:], mask9, AX_X, ALU.add)
                    settle()
                    v.reciprocal(stat[:], stat[:])
                    settle()
                    v.tensor_tensor(mask9, mask9, stat[:].unsqueeze(2).to_broadcast([P, BAND_SUBS * 2, TAPS]), ALU.mult)
                    settle()
                    cw = corner_w[:, i].rearrange("p t (s k) -> p t s k", k=4)
                    v.tensor_tensor(lower[:], mask[:], xy[:, :, :, 1], ALU.mult)
                    settle()
                    v.tensor_tensor(upper[:], mask[:], lower[:], ALU.subtract)
                    v.tensor_tensor(cw[:, :, :, 3], lower[:], xy[:, :, :, 0], ALU.mult)
                    settle()
                    v.tensor_tensor(cw[:, :, :, 1], upper[:], xy[:, :, :, 0], ALU.mult)
                    v.tensor_tensor(cw[:, :, :, 2], lower[:], cw[:, :, :, 3], ALU.subtract)
                    settle()
                    v.tensor_tensor(cw[:, :, :, 0], upper[:], cw[:, :, :, 1], ALU.subtract)
                    settle()
                elif what == "sample":
                    slot = gather_slot(i)
                    g, tt = divmod(i, BAND_SUBS)
                    each = 16 * SAMPLES
                    dve.wait_ge(gather_done[slot], n * (SLOT_USES[slot] * each) + (slot_use(i) + 1) * each)
                    dve.wait_ge(y_turned.sem, y_turned.free(n, i // 2, 2))
                    product = gathered[:, slot].rearrange("p (a c) -> p a c", c=CG)
                    v.tensor_tensor(product, product,
                                    corner_w[:, g, tt].unsqueeze(2).to_broadcast([P, SAMPLES * 4, CG]), ALU.mult)
                    settle()
                    v.tensor_reduce(y[:, i // 2 % 2, b].rearrange("p (g c) -> p g c", c=CG),
                                    product.rearrange("p (g k) c -> p g c k", g=2), AX_X, ALU.add)\
                        .then_inc(sampled.sem, 1)
                elif what == "turn":
                    wait(y_turned, n, i)
                    wait(mixed, n, i - 1)
                    v.tensor_copy(yT[:], chain_ps[:, :P]).then_inc(y_copied.sem, 1)
                elif what == "mix":
                    r = blk_rows(i)
                    wait(mixed, n, i)
                    dve.wait_ge(x_tok_in[b].sem, x_tok_in[b].after(n, i // 2))
                    wait(mid_turned, n, i - 1)
                    add_norm(chain_ps[:r, :C], mid, x_tok[:r, b], 0, r)
                    v.scalar_tensor_tensor(mid[:r], ln_a[:r], rstd[:r], ln_b[:r], ALU.mult, ALU.add)\
                        .then_inc(mid_ready.sem, 1)
                elif what == "turn_mid":
                    r = blk_rows(i)
                    wait(mid_turned, n, i)
                    wait(hid_done, n, i - 1)
                    v.tensor_copy(midT[:, :r], chain_ps[:, :r]).then_inc(mid_copied.sem, 1)
                elif what == "mlp_out":
                    r = blk_rows(i)
                    wait(mlp_done, n, i)
                    wait(quad_used, n, last_use(QUAD_INDEX, i))
                    add_norm(chain_ps[:r, :C], x1, mid[:r], 3, r)
                    v.scalar_tensor_tensor(x1[:r, x1_place(odd, i)], ln_a[:r], rstd[:r], ln_b[:r], ALU.mult, ALU.add)
                    settle()
                    moments(x1[:r, x1_place(odd, i)], r)
                    v.tensor_scalar(values[:r, value_place(odd, i), :C], x1[:r, x1_place(odd, i)], mv[:r, 0:1], rstd[:r], ALU.subtract, ALU.mult)\
                        .then_inc(norm_ready.sem, 1)
                elif what == "turn_norm":
                    r = blk_rows(i)
                    wait(norm_turned, n, i)
                    wait(keys_done, n, i - 1)
                    v.tensor_copy(lnT[:, :r], chain_ps[:, :r]).then_inc(norm_copied.sem, 1)
                elif what == "keys":
                    r = blk_rows(i)
                    wait(keys_done, n, i)
                    wait(tanh_done, n, last_use(UNIT_INDEX, i))
                    at = key_column(odd, i)
                    v.tensor_copy(key_rep[:, at:at + r], chain_ps[:, :r])
                    v.tensor_scalar(query[:, i * A:i * A + r // ROWS8], chain_ps[:, P:P + r // ROWS8], tiny[:, 0:1],
                                    None, ALU.add)
                    settle().then_inc(keys_copied.sem, 1)
                elif what == "mask":
                    r = blk_rows(i)
                    c = len(chunks_of(i)) - 1
                    ci, at = CHUNK_INDEX[i, c], column_in_chunk(odd, chunks_of(i)[c], i)
                    wait(exp_done, n, ci)
                    diagonal = expo[:r, ci % 2, at:at + r]
                    v.tensor_tensor(diagonal, diagonal, earlier[:r, :r], ALU.mult).then_inc(masked.sem, 1)
                elif what == "values":
                    k, c, q = name[1:]
                    r = blk_rows(k)
                    quad = chunks_of(k)[c][4 * q:4 * q + 4]
                    if quad:
                        pi = QUAD_INDEX[k, c, q]
                        wait(exp_turned, n, pi)
                        dve.wait_ge(quad_used.sem, quad_used.free(n, pi, 2))
                        for z, rows_ in column_runs(quad):
                            last = v.tensor_copy(expoT[:rows_, pi % 2, z[0]:z[1], :r],
                                                 turn_ps[:rows_, z[0]:z[1], :r])
                        if len(column_runs(quad)) > 1:
                            last = settle()
                        last.then_inc(exp_copied.sem, 1)
                elif what == "finish":
                    r = blk_rows(i)
                    wait(quad_used, n, QUAD_INDEX[i, len(chunks_of(i)) - 1, -(-len(chunks_of(i)[-1]) // 4) - 1])
                    dve.wait_ge(block_out[b].sem, block_out[b].after(n, i // 2 - 1))
                    wait(ln2_turned, n, i - 1)
                    v.tensor_scalar(den[:r, 0:1], value_ps[:r, C:C + 1], 1e-10, None, ALU.add)
                    settle()
                    v.reciprocal(den[:r, 1:2], den[:r, 0:1])
                    settle()
                    v.scalar_tensor_tensor(x2[:r, b], value_ps[:r, :C], den[:r, 1:2], x1[:r, x1_place(odd, i)],
                                           ALU.mult, ALU.add)
                    settle().then_inc(x2_ready.sem, 1)
                    moments(x2[:r, b], r)
                    v.tensor_scalar(xln2[:r, b], x2[:r, b], mv[:r, 0:1], rstd[:r], ALU.subtract, ALU.mult)\
                        .then_inc(ln2_ready.sem, 1)
                elif what == "route":
                    r = blk_rows(i)
                    wait(ln2_turned, n, i)
                    wait(logits_done, n, i - 1)
                    v.tensor_copy(xln2T[:, :r], side_ps[:, :r])\
                        .then_inc(ln2_copied.sem, 1)
                    settle().then_inc(side_read, 1)
                elif what == "logits":
                    r = blk_rows(i)
                    wait(logits_done, n, i)
                    v.tensor_scalar(logit[:, b, :r], side_ps[:E, :r], gate_b[:], None, ALU.add)\
                        .then_inc(logits_copied.sem, 1)
                    settle().then_inc(side_read, 1)

            walk(dve, "dve", task)

        @block.scalar
        def _(act):
            for ln in (h_ready, mask_exp, gelu_done, tanh_done, exp_done):
                nc.scalar.sem_inc(ln.sem, ln.lead)
            act.wait_ge(consts_ready, 1)

            def wait(ln, image, i):
                act.wait_ge(ln.sem, ln.after(image, i))

            def task(n, odd, name):
                what, i = name[:2]
                if what == "conv":
                    wait(conv_done, n, i)
                    wait(params_done, n, i - 1)
                    nc.scalar.activation(h_band[:], side_ps[:, :BAND], ACT.Gelu, bias=bn[:, 1:2], scale=bn[:, 0:1])\
                        .then_inc(h_ready.sem, 1)
                elif what == "offsets":
                    wait(mask_shifted, n, i)
                    nc.scalar.activation(mask[:], mask[:], ACT.Exp).then_inc(mask_exp.sem, 1)
                elif what == "hidden":
                    r = blk_rows(i)
                    wait(hid_done, n, i)
                    wait(mlp_done, n, i - 1)
                    nc.scalar.activation(hid[:, :, :r], chain_ps[:].rearrange("p (a b) -> p a b", b=P)[:, :, :r],
                                         ACT.Gelu).then_inc(gelu_done.sem, 1)
                elif what == "unit":
                    k, c, s = name[1:]
                    ui = UNIT_INDEX[k, c, s]
                    if (c, s) == (0, 0):
                        wait(keys_copied, n, k)
                    act.wait_ge(scored.sem, scored.free(n, ui, TANH_SLOTS))
                    tiles = chunks_of(k)[c]
                    w = chunk_width(tiles)
                    lo = key_column(odd, tiles[-1] if odd else tiles[0])
                    col = k * A + row_group(k, s)
                    nc.scalar.activation(tanh[:, ui % TANH_SLOTS, :w], key_rep[:, lo:lo + w], ACT.Tanh,
                                         bias=query[:, col:col + 1]).then_inc(tanh_done.sem, 1)
                elif what == "exp":
                    k, c = name[1:]
                    r = blk_rows(k)
                    ci = CHUNK_INDEX[k, c]
                    w = chunk_width(chunks_of(k)[c])
                    wait(scored, n, UNIT_INDEX[k, c, r // ROWS8 - 1])
                    wait(exp_turned, n, last_quad_of_chunk(ci - 2))
                    nc.scalar.activation(expo[:r, ci % 2, :w], score_ps[:r, ci % 2, :w], ACT.Exp, bias=tiny[:r, 2:3])\
                        .then_inc(exp_done.sem, 1)

            walk(act, "act", task)

        @block.tensor
        def _(pe):
            mm = nc.tensor.matmul
            for ln in (band_turned, in_projected, patch_turned, conv_done, params_done, y_turned, mixed, mid_turned,
                       hid_done, mlp_done, norm_turned, keys_done, scored, exp_turned, quad_used, ln2_turned,
                       logits_done):
                nc.tensor.sem_inc(ln.sem, ln.lead)
            pe.wait_ge(consts_ready, 1)
            side_uses = []
            earlier_uses = []
            last_conv = []

            def wait(ln, image, i):
                pe.wait_ge(ln.sem, ln.after(image, i))

            def side_free():
                if last_conv:
                    wait(h_ready, *last_conv.pop())
                if side_uses or not (isinstance(earlier_uses[-1], int) and earlier_uses[-1] == 0):
                    pe.wait_ge(side_read, earlier_uses[-1] + len(side_uses))
                side_uses.append(1)

            def turn(out, src, r, cols=P):
                if r < P or cols < P:
                    nc.tensor.sem_inc(pe_step, 1)
                return mm(out, src, ident[:r, :r], is_transpose=True, start=True, stop=True)

            def task(n, odd, name):
                what, i = name[:2]
                b = i % 2
                if what == "image_in":
                    side_free()
                    pe.wait_ge(x_band_in[b].sem, x_band_in[b].after(n, i // 2))
                    for q in range(4):
                        last = turn(side_ps[:, q * 112:(q + 1) * 112], x_band[:, b, q], 112)
                    last.then_inc(band_turned.sem, 1)
                elif what == "project_in":
                    side_free()
                    wait(band_copied, n, i)
                    mm(side_ps[:, :BAND], w_in[:], x_pad[:, 1 + i * BAND_ROWS:1 + (i + 1) * BAND_ROWS, 1:W + 1],
                       start=True, stop=True).then_inc(in_projected.sem, 1)
                elif what == "patches":
                    side_free()
                    wait(in_copied, n, min(NBAND - 1, ((i * P + P + HP) // HP - 1) // BAND_ROWS))
                    for k in range(4):
                        dy, dx = divmod(k, 2)
                        at = i * P + dy * HP + dx
                        last = turn(side_ps[:patch_rows(i), k * C:(k + 1) * C], xp_flat[:, at:at + patch_rows(i)], P,
                                    patch_rows(i))
                    last.then_inc(patch_turned.sem, 1)
                elif what == "conv":
                    side_free()
                    wait(band_copied, n, min(i + 1, NBAND - 1))
                    for t in range(TAPS):
                        dy, dx = divmod(t, 3)
                        last = mm(side_ps[:, :BAND], taps[:, t],
                                  x_pad[:, i * BAND_ROWS + dy:(i + 1) * BAND_ROWS + dy, dx:dx + W],
                                  start=t == 0, stop=t == TAPS - 1)
                    last.then_inc(conv_done.sem, 1)
                    side_uses.pop()
                    last_conv.append((n, i))
                elif what == "offsets":
                    side_free()
                    wait(h_ready, n, i)
                    for t in range(BAND_SUBS):
                        for half in range(2):
                            last = mm(side_ps[half * SUB:(half + 1) * SUB, t * PARAMS:(t + 1) * PARAMS],
                                      h_band[:, t * SUB:(t + 1) * SUB], w_par[:, half], start=True, stop=True)
                    last.then_inc(params_done.sem, 1)
                elif what == "turn":
                    wait(sampled, n, min(2 * i + 1, NSUB - 1))
                    wait(keys_copied, n, i - 1)
                    turn(chain_ps[:, :P], y[:, b].rearrange("p a b -> p (a b)"), P).then_inc(y_turned.sem, 1)
                elif what == "mix":
                    r = blk_rows(i)
                    wait(y_copied, n, i)
                    last = mm(chain_ps[:r, :C], ones[:, :r], rows[:, HID:HID + C], start=True, stop=False)
                    for s in range(r // SUB):
                        part = slice(s * SUB, (s + 1) * SUB)
                        for half in range(2):
                            last = mm(chain_ps[part, :C], yT[part, half * SUB:(half + 1) * SUB], w_out[part, half],
                                      start=False, stop=half == 1)
                    last.then_inc(mixed.sem, 1)
                elif what == "turn_mid":
                    r = blk_rows(i)
                    wait(mid_ready, n, i)
                    turn(chain_ps[:, :r], mid[:r], r).then_inc(mid_turned.sem, 1)
                elif what == "hidden":
                    r = blk_rows(i)
                    wait(mid_copied, n, i)
                    for c in range(HID // P):
                        cols = slice(c * P, (c + 1) * P)
                        mm(chain_ps[:, c * P:c * P + r], rows[:, cols], ones[:, :r], start=True, stop=False)
                        last = mm(chain_ps[:, c * P:c * P + r], w_fc1[:, cols], midT[:, :r], start=False, stop=True)
                    last.then_inc(hid_done.sem, 1)
                elif what == "mlp_out":
                    r = blk_rows(i)
                    wait(gelu_done, n, i)
                    mm(chain_ps[:r, :C], ones[:, :r], rows[:, HID + C:], start=True, stop=False)
                    for c in range(HID // P):
                        last = mm(chain_ps[:r, :C], hid[:, c, :r], w_fc2[:, c], start=False, stop=c == HID // P - 1)
                    last.then_inc(mlp_done.sem, 1)
                elif what == "turn_norm":
                    r = blk_rows(i)
                    wait(norm_ready, n, i)
                    turn(chain_ps[:, :r], values[:r, value_place(odd, i), :C], r).then_inc(norm_turned.sem, 1)
                elif what == "keys":
                    r = blk_rows(i)
                    wait(norm_copied, n, i)
                    mm(chain_ps[:, :r], w_key[:].rearrange("p a b -> p (a b)"), lnT[:, :r], start=True, stop=True)
                    for q in range(ROWS8):
                        last = mm(chain_ps[:, P:P + r // ROWS8], w_query[:, q].rearrange("p a b -> p (a b)"),
                                  lnT[:, q:r:ROWS8], start=q == 0, stop=q == ROWS8 - 1)
                    last.then_inc(keys_done.sem, 1)
                elif what == "unit":
                    k, c, s = name[1:]
                    r = blk_rows(k)
                    ui, ci = UNIT_INDEX[k, c, s], CHUNK_INDEX[k, c]
                    w = chunk_width(chunks_of(k)[c])
                    group = row_group(k, s)
                    col, place = divmod(group, 4)
                    if s == 0:
                        pe.wait_ge(exp_done.sem, exp_done.free(n, ci, 2))
                    wait(tanh_done, n, ui)
                    for lo in range(0, w, 512):
                        hi = min(w, lo + 512)
                        last = mm(score_ps[32 * col:32 * col + 32, ci % 2, lo:hi], score_w[:, place],
                                  tanh[:, ui % TANH_SLOTS, lo:hi], start=place == 0, stop=place == 3)
                    last.then_inc(scored.sem, 1)
                elif what == "values":
                    k, c, q = name[1:]
                    r = blk_rows(k)
                    tiles = chunks_of(k)[c]
                    ci = CHUNK_INDEX[k, c]
                    if q == 0:
                        wait(exp_done, n, ci)
                        if c == len(chunks_of(k)) - 1:
                            wait(masked, n, k)
                    if (k, c, q) in QUAD_INDEX:
                        pi = QUAD_INDEX[k, c, q]
                        pe.wait_ge(exp_copied.sem, exp_copied.after(n, pi - 1))
                        for z, j in enumerate(tiles[4 * q:4 * q + 4]):
                            at = column_in_chunk(odd, tiles, j)
                            wj = blk_rows(j)
                            last = turn(turn_ps[:wj, z, :r], expo[:r, ci % 2, at:at + wj], r, wj)
                        last.then_inc(exp_turned.sem, 1)
                    if q > 0:
                        pi = QUAD_INDEX[k, c, q - 1]
                        wait(exp_copied, n, pi)
                        if c == 0 and q == 1:
                            wait(x2_ready, n, k - 1)
                        for z, j in enumerate(tiles[4 * q - 4:4 * q]):
                            wj = blk_rows(j)
                            last = mm(value_ps[:r, :C + 1], expoT[:wj, pi % 2, z, :r], values[:wj, value_place(odd, j)],
                                      start=j == 0, stop=j == k)
                        last.then_inc(quad_used.sem, 1)
                elif what == "route":
                    r = blk_rows(i)
                    side_free()
                    wait(ln2_ready, n, i)
                    turn(side_ps[:, :r], xln2[:r, b], r).then_inc(ln2_turned.sem, 1)
                elif what == "logits":
                    r = blk_rows(i)
                    side_free()
                    wait(ln2_copied, n, i)
                    mm(side_ps[:E, :r], gate_w[:], xln2T[:, :r], start=True, stop=True).then_inc(logits_done.sem, 1)

            def begin(n):
                side_uses.clear()
                last_conv.clear()
                first = isinstance(n, int) and n < 1
                last = isinstance(n, int) and n == images
                if first:
                    earlier_uses.append(0 if n < 0 else side_uses_of[-1])
                else:
                    earlier_uses.append(n * sum(side_uses_of.values()) + (side_uses_of[-1] - side_uses_of[1]
                                        - (side_uses_of[-1] if last else 0)))
                if not last and not (first and n < 0):
                    age, i = last_conv_of_period
                    last_conv.append((n - 1 - age, i))

            walk(pe, "pe", task, begin)


def last_use(index, i):
    if i < EARLY:
        return max(at for (k, *_), at in index.items() if k == i) - len(index)
    return -1


def row_group(k, s):
    cols = blk_rows(k) // 32
    return 4 * (s % cols) + s // cols


def last_quad_of_chunk(ci):
    k, c = [kc for kc, i in CHUNK_INDEX.items() if i == ci % CHUNKS][0]
    return QUAD_INDEX[k, c, -(-len(chunks_of(k)[c]) // 4) - 1] - (QUADS if ci < 0 else 0)


def column_runs(quad):
    whole = sum(blk_rows(j) == P for j in quad)
    runs = [((0, whole), P)] if whole else []
    return runs + [((z, z + 1), blk_rows(quad[z])) for z in range(whole, len(quad))]


ROW_T = 28
ROW_P = S // ROW_T
SLOTS = 4
PER = 4
LOW = -3.0e38


def route_and_experts(nc, io, xln2_d, logits_d, chosen_d, expert_d, images):
    pairs = images * E // P
    with ExitStack() as ctx:
        def sb(name, shape, dt=F32):
            return ctx.enter_context(nc.sbuf_tensor(name, shape, dt))

        def ps(name, shape):
            return ctx.enter_context(nc.psum_tensor(name, shape, F32))

        def sem(name):
            return ctx.enter_context(nc.semaphore(name))

        eye = sb("eye", [P, P])
        bias1 = sb("bias1", [P, E, HID // P])
        score = sb("score", [P, 2, S])
        prob = sb("prob", [P, S])
        chosen = sb("chosen", [P, 2, S])
        chosenT = sb("chosenT", [ROW_P, ROW_T, P])
        tokens = sb("tokens", [ROW_P, 2, 2, ROW_T, C])
        top = sb("top", [P, K_TOP])
        neg = sb("neg", [P, 1])
        total = sb("total", [P, 2])
        pooled = sb("pooled", [C, E, images])
        w1 = sb("w1", [P, SLOTS, PER, HID])
        w2 = sb("w2", [P, SLOTS, PER, HID])
        pre = sb("pre", [P, 2, PER, HID // P, images])
        act1 = sb("act1", [P, 2, PER, HID // P, images])
        outs = sb("outs", [images, 2, PER, C])

        turned_ps = ps("turned_ps", [P, 2, 4, P])
        pool_ps = ps("pool_ps", [P, 2, 512])
        hid_ps = ps("hid_ps", [P, 2, 512])
        out_ps = ps("out_ps", [P, 2, 512])

        eye_in = sem("eye_in")
        score_in = [sem(f"score_in{i}") for i in range(2)]
        tokens_in = [sem(f"tokens_in{i}") for i in range(2)]
        chosen_out = [sem(f"chosen_out{i}") for i in range(2)]
        w_in = [sem(f"expert_w_in{i}") for i in range(SLOTS)]
        expert_out = [sem(f"expert_out{i}") for i in range(2)]
        top_ready = sem("top_ready")
        prob_ready = sem("prob_ready")
        prob_used = sem("prob_used")
        chosen_ready = sem("chosen_ready")
        chosen_turned = sem("chosen_turned")
        chosen_copied = sem("chosen_copied")
        pooled_done = sem("pooled_done")
        pooled_ready = sem("pooled_ready")
        hid_done = sem("expert_hid_done")
        pre_ready = sem("pre_ready")
        act_ready = sem("act_ready")
        out_done = sem("expert_out_done")
        out_copied = sem("out_copied")
        steps = E // PER
        rounds = steps // SLOTS
        TURNS = ROW_T // 4

        block = ctx.enter_context(nc.Block())

        @block.sync
        def _(sp):
            sp.dma_start(eye[:], io["ident"]).then_inc(eye_in, 16)
            sp.dma_start(bias1[:], io["weight1"][:, C, :].rearrange("e (p c) -> p e c", c=HID // P)).then_inc(eye_in, 16)

            def load_tokens(pr):
                b = pr % 2
                sp.dma_start(score[:, b], logits_d[pr * P:(pr + 1) * P, :]).then_inc(score_in[b], 16)
                for half in range(2):
                    at = (2 * pr + half) * S
                    sp.dma_start(tokens[:, b, half], xln2_d[at:at + S, :].rearrange("(p t) c -> p t c", t=ROW_T))\
                        .then_inc(tokens_in[b], 16)

            def load_experts(first, slot):
                sp.dma_start(w1[:, slot], io["weight1"][bass.ds(first, PER), :C, :].rearrange("e p h -> p e h"))\
                    .then_inc(w_in[slot], 16)
                sp.dma_start(w2[:, slot], io["weight2"][bass.ds(first, PER), :HID, :]
                             .rearrange("e (p c) o -> p e (c o)", c=HID // P)).then_inc(w_in[slot], 16)

            for pr in range(min(2, pairs)):
                load_tokens(pr)
            for slot in range(SLOTS):
                load_experts(slot * PER, slot)
            for pr in range(pairs):
                sp.wait_ge(chosen_ready, pr + 1)
                sp.dma_start(chosen_d[pr * P:(pr + 1) * P, :], chosen[:, pr % 2]).then_inc(chosen_out[pr % 2], 16)
                if pr + 2 < pairs:
                    sp.wait_ge(pooled_done, pr + 1)
                    load_tokens(pr + 2)
            def results(it, slot):
                sp.wait_ge(out_copied, it * SLOTS + (slot + 1))
                sp.dma_start(expert_d[bass.ds(it * (SLOTS * PER) + slot * PER, PER)].rearrange("e b o -> b e o"),
                             outs[:, slot % 2]).then_inc(expert_out[slot % 2], 16)

            with sp.Fori(0, rounds - 1) as it:
                for slot in range(SLOTS):
                    results(it, slot)
                    load_experts(it * (SLOTS * PER) + (SLOTS + slot) * PER, slot)
            for slot in range(SLOTS):
                results(rounds - 1, slot)
            for b in range(2):
                sp.wait_ge(expert_out[b], 16 * steps // 2)
                if b < pairs:
                    sp.wait_ge(chosen_out[b], 16 * ((pairs + 1 - b) // 2))

        @block.vector
        def _(dve):
            v = nc.vector

            def settle():
                return v.drain()

            for pr in range(pairs):
                b = pr % 2
                dve.wait_ge(score_in[b], 16 * (pr // 2 + 1))
                v.max(top[:], score[:, b])
                settle()
                v.tensor_scalar(neg[:], top[:, 0:1], -1.0, None, ALU.mult)
                settle().then_inc(top_ready, 1)
                if pr >= 2:
                    dve.wait_ge(chosen_turned, TURNS * (pr - 1))
                    dve.wait_ge(chosen_out[b], 16 * (pr // 2))
                v.match_replace(chosen[:, b], top[:], score[:, b], LOW)
                settle()
                v.tensor_tensor(chosen[:, b], score[:, b], chosen[:, b], ALU.not_equal)
                dve.wait_ge(prob_ready, pr + 1)
                v.reciprocal(total[:, 1:2], total[:, 0:1])
                settle()
                v.scalar_tensor_tensor(chosen[:, b], prob[:], total[:, 1:2], chosen[:, b], ALU.mult, ALU.mult)
                settle().then_inc(chosen_ready, 1)
                for q in range(TURNS):
                    u = pr * TURNS + q
                    dve.wait_ge(chosen_turned, u + 1)
                    if q == 0 and pr:
                        dve.wait_ge(pooled_done, pr)
                    v.tensor_copy(chosenT[:, 4 * q:4 * q + 4], turned_ps[:ROW_P, u % 2])
                    settle().then_inc(chosen_copied, 1)
                dve.wait_ge(pooled_done, pr + 1)
                for half in range(2):
                    v.tensor_copy(pooled[:, :, 2 * pr + half], pool_ps[:, half, :E])
                settle().then_inc(pooled_ready, 1)
            dve.wait_ge(eye_in, 32)
            with dve.Fori(0, rounds) as it:
                for s in range(SLOTS):
                    b = s % 2
                    dve.wait_ge(hid_done, it * SLOTS + (s + 1))
                    v.tensor_tensor(pre[:, b].rearrange("p e c b -> p (e c) b"),
                                    hid_ps[:, b, :PER * HID // P * images].rearrange("p (a b) -> p a b", b=images),
                                    bias1[:, bass.ds(it * (SLOTS * PER) + s * PER, PER), :]
                                    .rearrange("p e c -> p (e c)").unsqueeze(2)
                                    .to_broadcast([P, PER * HID // P, images]), ALU.add)
                    settle().then_inc(pre_ready, 1)
                    dve.wait_ge(out_done, it * SLOTS + (s + 1))
                    dve.wait_ge(expert_out[b], it * (16 * SLOTS // 2) + (16 * (s // 2)))
                    v.tensor_copy(outs[:, b].rearrange("p e o -> p (e o)"), out_ps[:images, b])
                    settle().then_inc(out_copied, 1)

        @block.scalar
        def _(act):
            for pr in range(pairs):
                act.wait_ge(top_ready, pr + 1)
                if pr:
                    act.wait_ge(chosen_ready, pr)
                nc.scalar.activation(prob[:], score[:, pr % 2], ACT.Exp, bias=neg[:], accum_out=total[:, 0:1])
                nc.scalar.drain().then_inc(prob_ready, 1)
            with act.Fori(0, rounds) as it:
                for s in range(SLOTS):
                    act.wait_ge(pre_ready, it * SLOTS + (s + 1))
                    nc.scalar.activation(act1[:, s % 2], pre[:, s % 2], ACT.Gelu).then_inc(act_ready, 1)

        @block.tensor
        def _(pe):
            mm = nc.tensor.matmul
            pe.wait_ge(eye_in, 32)
            for pr in range(pairs):
                b = pr % 2
                pe.wait_ge(chosen_ready, pr + 1)
                for q in range(TURNS):
                    u = pr * TURNS + q
                    if u >= 2:
                        pe.wait_ge(chosen_copied, u - 1)
                    for z in range(4):
                        last = mm(turned_ps[:ROW_P, u % 2, z], chosen[:, b, 4 * q + z::ROW_T], eye[:],
                                  is_transpose=True, start=True, stop=True)
                    last.then_inc(chosen_turned, 1)
                pe.wait_ge(chosen_copied, (pr + 1) * TURNS)
                pe.wait_ge(tokens_in[b], 32 * (pr // 2 + 1))
                if pr:
                    pe.wait_ge(pooled_ready, pr)
                for half in range(2):
                    for t in range(ROW_T):
                        last = mm(pool_ps[:, half, :E], tokens[:, b, half, t], chosenT[:, t, half * E:(half + 1) * E],
                                  start=t == 0, stop=t == ROW_T - 1)
                last.then_inc(pooled_done, 1)
            pe.wait_ge(pooled_ready, pairs)
            with pe.Fori(0, rounds) as it:
                for s in range(SLOTS):
                    b = s % 2
                    pe.wait_ge(w_in[s], it * 32 + 32)
                    for e in range(PER):
                        for c in range(HID // P):
                            col = (e * (HID // P) + c) * images
                            last = mm(hid_ps[:, b, col:col + images], w1[:, s, e, c::HID // P],
                                      pooled[:, bass.ds(it * (SLOTS * PER) + s * PER + e, 1), :]
                                      .rearrange("p e b -> p (e b)"), start=True, stop=True)
                    last.then_inc(hid_done, 1)
                    pe.wait_ge(act_ready, it * SLOTS + (s + 1))
                    if s >= 2:
                        pe.wait_ge(out_copied, it * SLOTS + (s - 1))
                    for e in range(PER):
                        for c in range(HID // P):
                            last = mm(out_ps[:images, b, e * C:(e + 1) * C], act1[:, b, e, c], 
                                      w2[:, s, e, c * C:(c + 1) * C], start=c == 0, stop=c == HID // P - 1)
                    last.then_inc(out_done, 1)


def combine(nc, io, x2_d, chosen_d, expert_d, out, images):
    with ExitStack() as ctx:
        def sb(name, shape, dt=F32):
            return ctx.enter_context(nc.sbuf_tensor(name, shape, dt))

        def sem(name):
            return ctx.enter_context(nc.semaphore(name))

        expert = sb("expert", [E, images, C])
        bias2 = sb("bias2", [E, C])
        picked = sb("picked", [E, 2, S])
        resid = sb("resid", [ROW_P, 2, ROW_T * C])
        mix_ps = ctx.enter_context(nc.psum_tensor("mix_ps", [P, 8, 512], F32))
        expert_in = sem("expert_in")
        image_in = [sem(f"image_in{i}") for i in range(2)]
        expert_ready = sem("expert_ready")
        mixed = sem("expert_mixed")
        added = sem("added")
        out_done = [sem(f"image_out{i}") for i in range(2)]
        QUADS = ROW_T // 4
        block = ctx.enter_context(nc.Block())

        @block.sync
        def _(sp):
            sp.dma_start(expert[:], expert_d).then_inc(expert_in, 16)
            sp.dma_start(bias2[:], io["weight2"][:, HID, :]).then_inc(expert_in, 16)
            for n in range(images):
                b = n % 2
                if n >= 2:
                    sp.wait_ge(added, QUADS * (n - 1))
                    sp.wait_ge(out_done[b], 16 * (n // 2))
                sp.dma_start(picked[:, b], chosen_d[n * E:(n + 1) * E, :]).then_inc(image_in[b], 16)
                sp.dma_start(resid[:, b], x2_d[n * S:(n + 1) * S, :].rearrange("(p t) c -> p (t c)", t=ROW_T))\
                    .then_inc(image_in[b], 16)

        @block.scalar
        def _(act):
            for n in range(images):
                act.wait_ge(added, QUADS * (n + 1))
                act.dma_start(out[n * S:(n + 1) * S, :].rearrange("(p t) c -> p (t c)", t=ROW_T), resid[:, n % 2])\
                    .then_inc(out_done[n % 2], 16)
            for b in range(2):
                act.wait_ge(out_done[b], 16 * ((images + 1 - b) // 2))

        @block.vector
        def _(dve):
            v = nc.vector
            dve.wait_ge(expert_in, 32)
            v.tensor_tensor(expert[:], expert[:], bias2[:, None, :].to_broadcast([E, images, C]), ALU.add)
            v.drain().then_inc(expert_ready, 1)
            for n in range(images):
                for q in range(QUADS):
                    dve.wait_ge(mixed, n * QUADS + q + 1)
                    part = resid[:, n % 2, q * 512:(q + 1) * 512]
                    v.tensor_tensor(part, part, mix_ps[:ROW_P, (n * QUADS + q) % 8], ALU.add).then_inc(added, 1)

        @block.tensor
        def _(pe):
            pe.wait_ge(expert_ready, 1)
            for n in range(images):
                pe.wait_ge(image_in[n % 2], 32 * (n // 2 + 1))
                for q in range(QUADS):
                    u = n * QUADS + q
                    if u >= 8:
                        pe.wait_ge(added, u - 7)
                    for z in range(4):
                        last = nc.tensor.matmul(mix_ps[:ROW_P, u % 8, z * C:(z + 1) * C],
                                                picked[:, n % 2, 4 * q + z::ROW_T], expert[:, n], start=True, stop=True)
                    last.then_inc(mixed, 1)


def layout(inputs):
    import numpy as np

    def f(name):
        return np.asarray(inputs[name], dtype=np.float32)

    half, pos = np.divmod(np.arange(P), SUB)
    place = np.arange(BAND_SUBS)[None, :] * SUB + pos[:, None]
    tap = np.arange(SAMPLES) % TAPS
    grid = np.zeros((P, BAND_SUBS, SAMPLES, 2), np.float32)
    grid[..., 0] = (place % W)[..., None] + tap // 3
    grid[..., 1] = (place // W)[..., None] + tap % 3
    base = (2 * half[:, None] + np.arange(SAMPLES)[None, :] // TAPS).astype(np.float32)
    score_place = np.zeros((P, 4, 32), np.float32)
    for r in range(4):
        for q in range(ROWS8):
            score_place[q * A:(q + 1) * A, r, 8 * r + q] = 1.0
    off = f("L0_conv_w_off").reshape(C, 2, 2 * SAMPLES)
    msk = f("L0_conv_w_msk").reshape(C, 2, SAMPLES)
    b_par = np.concatenate([f("L0_conv_b_off").reshape(2, -1), f("L0_conv_b_msk").reshape(2, -1)], 1)
    w_out = f("L0_conv_w_out").reshape(2, SUB, C).transpose(1, 0, 2)
    chan = ["b_in", "dw_b", "bn_g", "bn_b", "bn_m", "bn_v"]
    affine = ["ln1_g", "ln1_b", "gamma1", "ln2_g", "ln2_b", "gamma2"]
    w1 = f("L1_attn_W1")
    arrays = {
        "x": f("x").reshape(-1, C),
        "ident": np.eye(P, dtype=np.float32),
        "earlier": np.tril(np.ones((P, P), np.float32), -1),
        "score_place": score_place,
        "grid": grid.reshape(P, BAND_SUBS, 2 * SAMPLES),
        "base_index": base,
        "chan": np.stack([f("L0_conv_" + n) for n in chan], 1),
        "dw": f("L0_conv_dw_w").reshape(C, TAPS),
        "w_in": f("L0_conv_w_in"),
        "w_par": np.concatenate([off, msk], 2),
        "b_par": np.repeat(b_par, SUB, 0),
        "w_out": np.concatenate([w_out, w_out], 0),
        "w_fc1": f("L0_conv_w_fc1"),
        "w_fc2": f("L0_conv_w_fc2").reshape(HID // P, P, C).transpose(1, 0, 2),
        "rows": np.concatenate([f("L0_conv_b_fc1"), f("L0_conv_b_out"), f("L0_conv_b_fc2")])[None],
        "affine": np.tile(np.stack([f("L0_conv_" + n) for n in affine])[None], (P, 1, 1)),
        "w_key": np.tile(w1[C:, None, :], (1, ROWS8, 1)),
        "w_q": w1[:C],
        "tiny": np.stack([np.tile(f("L1_attn_b1"), ROWS8), np.tile(f("L1_attn_w2")[:, 0], ROWS8),
                          np.tile(f("L1_attn_b2"), P)], 1),
        "gate_w": f("L1_ffn_gate_w").T,
        "gate_b": f("L1_ffn_gate_b")[:, None],
        "weight1": f("L1_ffn_weight1"),
        "weight2": f("L1_ffn_weight2"),
    }
    return {k: np.ascontiguousarray(a) for k, a in arrays.items()}


def program(nc, io, out, images):
    x2_d = nc.dram_tensor("x2_d", [images * S, C], F32, kind="Internal").ap()
    xln2_d = nc.dram_tensor("xln2_d", [images * S, C], F32, kind="Internal").ap()
    logits_d = nc.dram_tensor("logits_d", [images * E, S], F32, kind="Internal").ap()
    chosen_d = nc.dram_tensor("chosen_d", [images * E, S], F32, kind="Internal").ap()
    patches_d = [nc.dram_tensor(f"patches_{parity}", [PATCHES, GROUPS * 4 * CG], F32, kind="Internal").ap()
                 for parity in ("even", "odd")]
    expert_d = nc.dram_tensor("expert_d", [E, images, C], F32, kind="Internal").ap()
    first_layer_and_attention(nc, io, x2_d, xln2_d, logits_d, patches_d, images)
    route_and_experts(nc, io, xln2_d, logits_d, chosen_d, expert_d, images)
    combine(nc, io, x2_d, chosen_d, expert_d, out, images)


def kernel(**inputs):
    import numpy as np
    import concourse.bacc as bacc
    from concourse.bass_utils import run_bass_kernel_spmd as run

    images = inputs["x"].shape[0]
    arrays = layout(inputs)
    nc = bacc.Bacc("TRN2", target_bir_lowering=False, num_devices=1)
    io = {k: nc.dram_tensor(f"in_{k}", a.shape, F32, kind="ExternalInput").ap() for k, a in arrays.items()}
    out = nc.dram_tensor("out_x", (images * S, C), F32, kind="ExternalOutput").ap()
    program(nc, io, out, images)
    r = run(nc, [{f"in_{k}": a for k, a in arrays.items()}], core_ids=[0])
    return np.asarray(r.results[0]["out_x"]).reshape(inputs["x"].shape)
```
